# Optimizing a Trainium2 kernel written in Bass

```python
import numpy as np
import jax
import jax.numpy as jnp

def _softmax(x, axis=-1):
    return jax.nn.softmax(x, axis=axis)
def _gelu(x):
    return jax.nn.gelu(x, approximate=True)
def _silu(x):
    return jax.nn.silu(x)
def _sigmoid(x):
    return jax.nn.sigmoid(x)
def _layernorm(x, axis=-1, eps=1e-5):
    m = jnp.mean(x, axis=axis, keepdims=True)
    v = jnp.var(x, axis=axis, keepdims=True)
    return (x - m) / jnp.sqrt(v + eps)
def _scatter_add(tgt, idx, src, axis=0):
    return tgt.at[idx].add(src)
def _segment_sum(src, seg, n):
    return jax.ops.segment_sum(src, seg, n)

kernel_name = 'mk_conv_preact_d2_conv_nchw64_23bea6'

def setup_inputs(seed: int = 0):
    np.random.seed(seed)
    _w = jnp.asarray
    def _rec_inputs():
        import jax
        import jax.numpy as jnp
        _gk = jax.random.key(seed)
        x = -0.0003929 + 0.9999 * jax.random.normal(jax.random.fold_in(_gk, 1), (256, 64, 32, 32), jnp.float32)
        return x
    x = _rec_inputs()
    def _L0_conv_setup():
        import jax, jax.numpy as jnp
        import numpy as np
        B, T = (4, 64)
        HID = 64
        HT, WD = (32, 32)

        def log_g(x):
            return jnp.where(x >= 0, jnp.log(jnp.maximum(x, 0) + 0.5), -jax.nn.softplus(-x))
        key = jax.random.key(seed)
        k1, k2, k3 = jax.random.split(key, 3)
        x = jax.random.normal(k1, (B * T, HID, HT, WD), dtype=jnp.float32)
        conv_w = jax.random.normal(k2, (3 * HID, HID, 3, 3), dtype=jnp.float32) * 0.05
        conv_b = jax.random.normal(k3, (3 * HID,), dtype=jnp.float32) * 0.05
        h0 = jnp.zeros((B, HID, HT, WD), dtype=jnp.float32)
        return {'x': x, 'conv_w': conv_w, 'conv_b': conv_b, 'h0': h0}
    _L0_conv_all = _L0_conv_setup()
    _L0_conv_in = {k: v for k, v in _L0_conv_all.items() if k in ('conv_w', 'conv_b', 'h0', )}
    del _L0_conv_all

    def _L1_conv_setup():
        import jax, jax.numpy as jnp
        import numpy as np
        EPS = 0.001
        key = jax.random.key(seed)
        k1, k2 = jax.random.split(key)
        B, C, W, H = (16, 64, 256, 256)
        x = jax.random.normal(k1, (B, C, W, H), dtype=jnp.float32)
        keep = (jax.random.uniform(k2, (B, W, H)) < 0.3).astype(jnp.float32)
        x = x * keep[:, None, :, :]
        return {'x': x}
    _L1_conv_all = _L1_conv_setup()
    _L1_conv_in = {k: v for k, v in _L1_conv_all.items() if k in ()}
    del _L1_conv_all

    return {
        "x": x,
        "L0_conv_conv_w": _L0_conv_in["conv_w"],
        "L0_conv_conv_b": _L0_conv_in["conv_b"],
        "L0_conv_h0": _L0_conv_in["h0"],
    }

def reference(x, L0_conv_conv_w, L0_conv_conv_b, L0_conv_h0):
    import jax
    import jax.numpy as jnp
    def _L0_conv_ref(x, conv_w, conv_b, h0):
        import jax, jax.numpy as jnp
        import numpy as np
        B, T = (4, 64)
        HID = 64
        HT, WD = (32, 32)

        def log_g(x):
            return jnp.where(x >= 0, jnp.log(jnp.maximum(x, 0) + 0.5), -jax.nn.softplus(-x))
        y = jax.lax.conv_general_dilated(x, conv_w, window_strides=(1, 1), padding=((1, 1), (1, 1)), dimension_numbers=('NCHW', 'OIHW', 'NCHW')) + conv_b[None, :, None, None]
        y = y.reshape(B, T, 3 * HID, HT, WD)
        f_gate, i_gate, h_tilde = jnp.split(y, 3, axis=2)
        diff = f_gate - i_gate
        log_f = jax.nn.log_sigmoid(diff)
        log_i = log_f - diff
        log_h0 = log_g(h0[:, None])
        log_values = jnp.concatenate([log_h0, log_i + log_g(h_tilde)], axis=1)
        a_star = jnp.pad(jnp.cumsum(log_f, axis=1), ((0, 0), (1, 0), (0, 0), (0, 0), (0, 0)))
        log_h = a_star + jax.lax.cumlogsumexp(log_values - a_star, axis=1)
        out = jnp.exp(log_h)[:, 1:]
        return out.reshape(B * T, HID, HT, WD)

    def _L1_conv_ref(x):
        import jax, jax.numpy as jnp
        import numpy as np
        EPS = 0.001
        """Faithful masked batchnorm (training mode, affine=False).

            Original: per-batch nonzero() of channel-sum, pad index lists to the max
            count with zeros (i.e. duplicate location (0,0)), gather [B, Nmax, C],
            compute per-channel mean/var over ALL gathered entries (padding included),
            divide by sqrt(var+eps) (mean NOT subtracted in output), scatter back to
            nonzero locations — padded rows also overwrite location (0,0).
            """
        B, C, W, H = x.shape
        x1 = x.sum(axis=1)
        m = x1 != 0
        mf = m.astype(x.dtype)
        n = mf.sum(axis=(1, 2))
        Nmax = n.max()
        pad = Nmax - n
        total = (B * Nmax).astype(x.dtype)
        x00 = x[:, :, 0, 0]
        sum_c = jnp.einsum('bcwh,bwh->c', x, mf) + jnp.einsum('bc,b->c', x00, pad)
        mean = sum_c / total
        d = x - mean[None, :, None, None]
        var = (jnp.einsum('bcwh,bwh->c', d * d, mf) + jnp.einsum('bc,b->c', (x00 - mean[None, :]) ** 2, pad)) / total
        inv = 1.0 / jnp.sqrt(var + EPS)
        xn = x * inv[None, :, None, None]
        out = jnp.where(m[:, None, :, :], xn, x)
        has_pad = (pad > 0)[:, None]
        out = out.at[:, :, 0, 0].set(jnp.where(has_pad, x00 * inv[None, :], out[:, :, 0, 0]))
        return out

    def _gn(v, G=32, eps=1e-5):
        B_, C_, H_, W_ = v.shape
        g = v.reshape(B_, G, C_ // G, H_, W_)
        m = jnp.mean(g, axis=(2, 3, 4), keepdims=True)
        s = jnp.var(g, axis=(2, 3, 4), keepdims=True)
        return ((g - m) / jnp.sqrt(s + eps)).reshape(v.shape)

    def _ln_c(v, eps=1e-6):
        m = jnp.mean(v, axis=1, keepdims=True)
        s = jnp.var(v, axis=1, keepdims=True)
        return (v - m) / jnp.sqrt(s + eps)

    def _ln_t(v, eps=1e-5):
        m = jnp.mean(v, axis=-1, keepdims=True)
        s = jnp.var(v, axis=-1, keepdims=True)
        return (v - m) / jnp.sqrt(s + eps)

    def _to_tokens(v):
        B_, C_, H_, W_ = v.shape
        return v.reshape(B_, C_, H_ * W_).transpose(0, 2, 1)
    def _from_tokens(t, like):
        B_, C_, H_, W_ = like.shape
        return t.transpose(0, 2, 1).reshape(B_, C_, H_, W_)

    x = x + _L0_conv_ref(_gn(x), L0_conv_conv_w, L0_conv_conv_b, L0_conv_h0)
    x = x + _L1_conv_ref(_gn(x))
    return x


_drawn_inputs = setup_inputs


def setup_inputs(seed=0):
    import zlib

    import numpy as np

    out = dict(_drawn_inputs(seed))
    spreads = {'L0_conv_h0': (0.0, 0.8)}
    factors = {}
    for name, (base, spread) in spreads.items():
        noise = np.random.default_rng([zlib.crc32(name.encode()), seed]).standard_normal(out[name].shape)
        drawn = base * np.exp(spread * noise) if base else spread * noise
        out[name] = jnp.asarray(drawn.astype(out[name].dtype))
    for name, factor in factors.items():
        out[name] = (out[name] * factor).astype(out[name].dtype)
    return out
```

```python
import concourse.bass as bass
from concourse import mybir
from contextlib import ExitStack


SEQS, STEPS, CH, SIDE = 4, 64, 64, 32
PX = SIDE * SIDE
PAD = SIDE + 2
PP = PAD * PAD
HALF = PX // 2
ROWS = SIDE // 2
TAPS = 9
GROUPS = STEPS
TILES = 2
NT = GROUPS * TILES
XRING = 4
GN_EPS, BN_EPS = 1e-5, 1e-3
XSCALE = 512.0
WSCALE = 4096.0
COPIES = 8
PASSES = [(0, t, t) for t in range(9)] + [(1, t, t + 3) for t in range(3)] + [(1, t, t) for t in range(6, 9)]
K_S1, K_S2, K_MEAN, K_RSTD, K_FIRST, K_COUNT, K_END = 0, 2, 4, 6, 8, 10, 11

C_IDENT, C_PAIR, C_FOLD, C_SPREAD, C_OWN, C_ALL, C_ROW, C_SUM, C_FIRST, C_END = (
    0, 128, 256, 384, 896, 1152, 1664, 1792, 1824, 1825)


def constant_table():
    import numpy as np

    t = np.zeros((128, C_END), np.float32)
    p = np.arange(128)
    t[:, C_IDENT:C_IDENT + 128] = p[:, None] == p[None]
    t[:, C_PAIR:C_PAIR + 128] = 0.5 * (p[:, None] // 2 == p[None] // 2)
    t[:, C_FOLD:C_FOLD + 128] = p[:, None] % CH == p[None] % CH
    for chunk in range(4):
        for image in range(2):
            row = 32 * chunk + image
            own = p // CH == image
            t[row, C_SPREAD + 128 * chunk:][:128] = own
            t[row, C_OWN + 128 * (chunk // 2):][:128] = own
            t[row, C_ALL + 128 * (2 * (chunk // 2) + image):][:128] = 1.0
            t[row, C_ROW + 64 * (chunk // 2) + image] = 1.0
            t[64 * (chunk // 2) + image, C_FIRST] = 1.0
    for image in range(2):
        t[image * CH:(image + 1) * CH, C_SUM + image] = 1.0
    return t


class At:

    def __init__(self, i, plus, times=4):
        self.i, self.plus, self.times = i, plus, times

    def __add__(self, n):
        return At(self.i, self.plus + n, self.times)

    def exists(self):
        return self.i is not None or 0 <= self.plus < GROUPS

    def value(self, each, more=0):
        known = each * self.plus + more
        return known if self.i is None else self.i * (each * self.times) + known

    def round(self, ring, each, more=0):
        known = each * (self.plus // ring) + more
        return known if self.i is None else self.i * (each * (self.times // ring)) + known

    def done(self, each):
        return self.value(each, each) if self.i is not None else each * min(self.plus + 1, GROUPS)

    def slot(self, ring):
        return self.plus % ring


def wait(engine, semaphore, value):
    if not isinstance(value, int) or value > 0:
        engine.wait_ge(semaphore, value)


def preact_kernel(nc, x, conv_w, conv_b, h0, table, out, x1_dram, mask_dram):
    f32, f16, bf16, i32 = mybir.dt.float32, mybir.dt.float16, mybir.dt.bfloat16, mybir.dt.int32
    ALU = mybir.AluOpType
    ACT = mybir.ActivationFunctionType
    AX = mybir.AxisListType.X

    x_v = x.rearrange("(b t) c h w -> b t c (h w)", b=SEQS)
    out_v = out.rearrange("(b t) c h w -> b t c (h w)", b=SEQS)
    h0_v = h0.rearrange("b c h w -> b c (h w)")
    w_v = conv_w.rearrange("o c h w -> o (c h w)")
    b_v = conv_b.rearrange("(g o a) -> g o a", g=3, a=1)

    ctx = ExitStack()
    with ctx:
        def sb(name, shape, dt=f32):
            return ctx.enter_context(nc.sbuf_tensor(name, shape, dt))

        def sem(name):
            return ctx.enter_context(nc.semaphore(name))

        consts = sb("consts", [128, C_END])
        spread = sb("spread", [128, 4, 128], bf16)
        ident16 = sb("ident16", [128, 128], f16)
        wst = sb("wst", [128, 15, 128], f16)
        bias = sb("bias", [128, 1])
        bias_half = sb("bias_half", [128, 1])
        unscale = sb("unscale", [128, 1])
        X = sb("X", [128, XRING * TILES, PX])
        XN = sb("XN", [128, TILES, PX])
        XH = sb("XH", [128, TILES, PP], f16)
        XL = sb("XL", [128, TILES, PP], f16)
        U = sb("U", [128, 8, PP], f16)
        Z = sb("Z", [128, 8, PP], f16)
        F = sb("F", [128, TILES, PX])
        S = sb("S", [128, TILES, PX])
        Tc = sb("Tc", [128, TILES, PX])
        H = sb("H", [128, TILES, 2, PX])
        Y = sb("Y", [128, TILES, PX])
        MK = sb("MK", [128, 4, HALF], bf16)
        bn1 = sb("bn1", [128, TILES, 12])
        bn2 = sb("bn2", [128, TILES, 12])
        mv1 = sb("mv1", [128, TILES, 2])
        mv2 = sb("mv2", [128, TILES, 2])
        mg1 = sb("mg1", [128, TILES])
        dm1 = sb("dm1", [128, TILES])
        dm2 = sb("dm2", [128, TILES])
        ve1 = sb("ve1", [128, TILES])
        ve2 = sb("ve2", [128, TILES])
        pw1 = sb("pw1", [128, TILES])
        r1 = sb("r1", [128, TILES])
        power = sb("power", [128, TILES])
        xscale = sb("xscale", [128, TILES])
        idle = sb("idle", [128, 2])
        keep = sb("keep", [128, 4, K_END])
        kept = sb("kept", [128, GROUPS, K_END])
        small = sb("small", [128, 9])
        end = sb("end", [128, 12])
        counts = sb("counts", [128, 7, GROUPS])
        padn = sb("padn", [128, GROUPS, TILES])
        prod = sb("prod", [128, GROUPS, TILES])
        first = sb("first", [128, GROUPS])
        coef_a = sb("coef_a", [128, GROUPS, TILES])
        coef_b = sb("coef_b", [128, GROUPS, TILES])
        coef_c = sb("coef_c", [128, GROUPS, TILES])

        conv = ctx.enter_context(nc.psum_tensor("conv", [128, 2, PX], f32))
        bcast = ctx.enter_context(nc.psum_tensor("bcast", [128, PX], f32))
        sums = ctx.enter_context(nc.psum_tensor("sums", [128, HALF], f32))
        stat = ctx.enter_context(nc.psum_tensor("stat", [128, HALF], f32))

        names = """consts_in h0_in weights_in prep zeroed transposed split_ready setup_done h_init
            xn_ready xh_ready xl_ready conv_done evac_done g_ready fh_ready h_ready x1_ready
            bn1_done bn2_done st1_ready st2_ready avg1_done avg2_done link1 link2 ve1_ready ve2_ready pw1_done
            r1_ready r2_ready y_ready sums_done mask_ready bc_done ym_ready sq_done stored
            counts_ready counts_out fold folded pow_in pow_out coef_ready
            bc2_done t_done w_done first_fixed out_ready""".split()
        s = {n: sem(n) for n in names}
        loaded = [sem(f"loaded{n}") for n in range(XRING)]
        moved = [[sem(f"moved{p}{k}") for k in range(TILES)] for p in range(2)]
        mask_out = [sem(f"mask_out{p}") for p in range(2)]
        out_stored = [sem(f"out_stored{p}") for p in range(2)]
        back_in = [sem(f"back_in{n}") for n in range(XRING)]

        def wprep(p):
            return conv[:, 0, :].bitcast(f16)[:, 128 * p:128 * (p + 1)]

        def result(g, k):
            return (F, S)[g.slot(2)][:, k, :]

        def step_of(v, g):
            if g.i is None:
                return v[g.plus]
            return v[bass.ds(g.value(1), 1)].rearrange("a c p -> (a c) p")

        def kept_of(g, column=None, t=kept):
            cols = slice(None) if column is None else slice(column, column + 1)
            if g.i is None:
                return t[:, g.plus, cols]
            return t[:, bass.ds(g.value(1), 1), cols].rearrange("p a b -> p (a b)")

        inner = lambda t, k: t[:, k, :].rearrange("p (a b) -> p a b", b=PAD)[:, 1:1 + SIDE, 1:1 + SIDE]
        square = lambda ap: ap.rearrange("p (a b) -> p a b", b=SIDE)
        rows_of = lambda image: slice(CH * image, CH * (image + 1))

        block = ctx.enter_context(nc.Block())

        @block.sync
        def _(sp):
            sp.dma_start(consts[:, :], table).then_inc(s["consts_in"], 16)

            def wait_all(*pairs):
                pairs = [(semaphore, v if isinstance(v, int) else sp.snap(sp.to_reg(v))) for semaphore, v in pairs]
                sp.wait_ge(s["consts_in"], 16)
                for semaphore, value in pairs:
                    wait(sp, semaphore, value)

            taps = CH * TAPS
            sp.dma_start(X[0:CH, 6, 0:taps], w_v[0:CH, :]).then_inc(s["weights_in"], 16)
            sp.dma_start(X[0:CH, 7, 0:taps], w_v[CH:2 * CH, :]).then_inc(s["weights_in"], 16)
            sp.dma_start(X[CH:128, 6, 0:taps], w_v[2 * CH:3 * CH, :]).then_inc(s["weights_in"], 16)
            sp.dma_start(small[0:CH, 0:1], b_v[0]).then_inc(s["weights_in"], 16)
            sp.dma_start(small[0:CH, 1:2], b_v[1]).then_inc(s["weights_in"], 16)
            sp.dma_start(small[CH:128, 0:1], b_v[2]).then_inc(s["weights_in"], 16)

            def load(g):
                if not g.exists():
                    return
                wait_all((s["y_ready"], (g + -XRING).value(TILES, TILES)),
                         (s["stored"], (g + -XRING).value(64, 64)))
                for seq in range(SEQS):
                    slot = TILES * g.slot(XRING) + seq // 2
                    sp.dma_start(X[rows_of(seq % 2), slot, :], step_of(x_v[seq], g))\
                        .then_inc(loaded[g.slot(XRING)], 16)

            def copies(g, k):
                if not g.exists():
                    return
                wait_all((s["xl_ready"], g.value(TILES, k + 1)),
                         (s["conv_done"], (g + -2).value(4, 2 * k + 2)))
                done = moved[g.slot(2)][k]
                for image in range(2):
                    slot, half = 4 * g.slot(2) + 2 * k + image, rows_of(image)
                    high, low = XH[half, k, :], XL[half, k, :]
                    n = SIDE * PAD
                    sp.dma_start(U[0:CH, slot, :], high).then_inc(done, 16)
                    sp.dma_start(U[CH:128, slot, :], low).then_inc(done, 16)
                    sp.dma_start(Z[0:CH, slot, 0:n], high[:, 0:n]).then_inc(done, 16)
                    sp.dma_start(Z[CH:128, slot, 0:n], high[:, PAD:PAD + n]).then_inc(done, 16)

            def store(g):
                if not g.exists():
                    return
                wait_all((s["x1_ready"], g.value(TILES, TILES)))
                for seq in range(SEQS):
                    slot = TILES * g.slot(XRING) + seq // 2
                    sp.dma_start(step_of(x1_dram[seq], g), X[rows_of(seq % 2), slot, :]).then_inc(s["stored"], 16)

            def store_mask(g):
                if not g.exists():
                    return
                wait_all((s["mask_ready"], g.value(1, 1)))
                for chunk in range(4):
                    to = mask_dram[chunk]
                    sp.dma_start(step_of(to, g), MK[32 * chunk:32 * chunk + 2, g.slot(2), :])\
                        .then_inc(mask_out[g.slot(2)], 16)

            def step(g):
                copies(g + 1, 0)
                copies(g + 1, 1)
                store(g + -1)
                store_mask(g + -2)
                load(g + 3)

            load(At(None, 0))
            load(At(None, 1))
            for seq in range(SEQS):
                sp.dma_start(H[rows_of(seq % 2), seq // 2, 1, :], h0_v[seq]).then_inc(s["h0_in"], 16)
            wait(sp, s["setup_done"], 1)
            for n in range(-1, 4):
                step(At(None, n))
            with sp.Fori(0, 14) as i:
                for q in range(4):
                    step(At(i, 4 + q))
            for n in range(60, GROUPS + 2):
                step(At(None, n))

            sp.wait_ge(s["stored"], 64 * GROUPS)
            for p in range(2):
                sp.wait_ge(mask_out[p], 64 * (GROUPS // 2))
            sp.wait_ge(s["y_ready"], NT)
            sp.wait_ge(s["bc_done"], NT)

            def fetch(g):
                if not g.exists():
                    return
                before = (g + -XRING).value(TILES, TILES)
                wait_all((s["t_done"], before), (s["w_done"], before), (s["bc2_done"], before))
                done = back_in[g.slot(XRING)]
                for seq in range(SEQS):
                    slot = TILES * g.slot(XRING) + seq // 2
                    sp.dma_start(X[rows_of(seq % 2), slot, :], step_of(x1_dram[seq], g)).then_inc(done, 16)
                for chunk in range(4):
                    sp.dma_start(MK[32 * chunk:32 * chunk + 2, g.slot(XRING), :], step_of(mask_dram[chunk], g))\
                        .then_inc(done, 16)

            def put(g):
                if not g.exists():
                    return
                wait_all((s["out_ready"], g.value(TILES, TILES)))
                for seq in range(SEQS):
                    slot = result(g, seq // 2)
                    sp.dma_start(step_of(out_v[seq], g), slot[rows_of(seq % 2), :])\
                        .then_inc(out_stored[g.slot(2)], 16)

            for n in range(3):
                fetch(At(None, n))
            for n in range(4):
                fetch(At(None, n + 3))
                put(At(None, n))
            with sp.Fori(0, 14) as i:
                for q in range(4):
                    fetch(At(i, 7 + q))
                    put(At(i, 4 + q))
            for n in range(60, GROUPS):
                fetch(At(None, n + 3))
                put(At(None, n))
            for p in range(2):
                sp.wait_ge(out_stored[p], 64 * (GROUPS // 2))

        @block.tensor
        def _(pe):
            mm = nc.tensor.matmul
            pe.wait_ge(s["split_ready"], 1)
            split = XN[:, 0, :].bitcast(f16)
            for p, (low, first_tap, next_tap) in enumerate(PASSES):
                part = split[:, low * 1024:low * 1024 + CH * TAPS].rearrange("p (c t) -> p t c", t=TAPS)
                for n, tap in enumerate((first_tap, next_tap)):
                    last = nc.tensor.transpose(wprep(p)[CH * n:CH * (n + 1), :], part[:, tap, :], ident16[:, :])
            last.then_inc(s["transposed"], 1)
            pe.wait_ge(s["setup_done"], 1)

            def unit(g, k, image):
                if not g.exists():
                    return
                if image == 0:
                    wait(pe, moved[g.slot(2)][k], g.round(2, 16 * COPIES, 16 * COPIES))
                wait(pe, s["evac_done"], g.value(4, 2 * k + image - 1))
                slot = 4 * g.slot(2) + 2 * k + image
                for p, (low, tap, _) in enumerate(PASSES):
                    operand = Z if 9 <= p < 12 else U
                    ky, kx = divmod(tap, 3)
                    padded = operand[:, slot, :].rearrange("p (a b) -> p a b", b=PAD)
                    for h in range(2):
                        at = h * ROWS + ky
                        last = mm(conv[:, image, h * HALF:(h + 1) * HALF], wst[:, p, :],
                                  padded[:, at:at + ROWS, kx:kx + SIDE], start=(p == 0), stop=(p == len(PASSES) - 1))
                last.then_inc(s["conv_done"], 1)

            def average(g, mv, ready, to, done, read1, read2):
                if not g.exists():
                    return
                wait(pe, s[ready], g.done(1))
                wait(pe, s["ve1_ready"], read1)
                wait(pe, s["ve2_ready"], read2)
                mm(stat[:, to:to + 4], consts[:, C_PAIR:C_PAIR + 128], mv[:, :, :].rearrange("p k m -> p (k m)"),
                   start=True, stop=True).then_inc(s[done], 1)

            def channel_sums(g):
                if not g.exists():
                    return
                wait(pe, s["y_ready"], g.value(TILES, TILES))
                wait(pe, s["mask_ready"], g.value(1, 0))
                for chunk in range(4):
                    k, h = divmod(chunk, 2)
                    last = mm(sums[32 * chunk:32 * chunk + 32, :], consts[:, C_SUM:C_SUM + 32],
                              Y[:, k, h * HALF:(h + 1) * HALF], start=True, stop=True)
                last.then_inc(s["sums_done"], 1)

            def spread_mask(g, k):
                if not g.exists():
                    return
                wait(pe, s["mask_ready"], g.value(1, 1))
                wait(pe, s["ym_ready"], g.value(TILES, k))
                for h in range(2):
                    last = mm(bcast[:, h * HALF:(h + 1) * HALF], spread[:, 2 * k + h, :], MK[:, g.slot(2), :],
                              start=True, stop=True)
                last.then_inc(s["bc_done"], 1)

            def step(g):
                unit(g, 0, 0)
                channel_sums(g + -2)
                unit(g, 0, 1)
                average(g + -1, mv2, "st2_ready", 4, "avg2_done", (g + 1).done(1), (g + -2).done(1))
                spread_mask(g + -2, 0)
                unit(g, 1, 0)
                average(g + 2, mv1, "st1_ready", 0, "avg1_done", (g + 1).done(1), (g + -1).done(1))
                spread_mask(g + -2, 1)
                unit(g, 1, 1)

            for n in range(-2, 4):
                step(At(None, n))
            with pe.Fori(0, 14) as i:
                for q in range(4):
                    step(At(i, 4 + q))
            for n in range(60, GROUPS + 2):
                step(At(None, n))

            pe.wait_ge(s["counts_ready"], 1)
            for n in range(6):
                mm(stat[:, GROUPS * n:GROUPS * (n + 1)], consts[:, C_OWN + 128 * n:C_OWN + 128 * (n + 1)],
                   kept[:, :, K_COUNT], start=True, stop=True)
            mm(stat[:, GROUPS * 6:GROUPS * 7], consts[:, C_ROW:C_ROW + 128], kept[:, :, K_COUNT],
               start=True, stop=True).then_inc(s["counts_out"], 1)
            pe.wait_ge(s["fold"], 1)
            mm(sums[:, 0:2], consts[:, C_FOLD:C_FOLD + 128], end[:, 4:6], start=True, stop=True)\
                .then_inc(s["folded"], 1)

            def spread_again(g):
                for k in range(TILES):
                    if k == 0:
                        wait(pe, s["first_fixed"], g.value(1, 1))
                    wait(pe, s["t_done"], g.value(TILES, k - 1))
                    for h in range(2):
                        last = mm(conv[:, k, h * HALF:(h + 1) * HALF], spread[:, 2 * k + h, :],
                                  MK[:, g.slot(XRING), :], start=True, stop=True)
                    last.then_inc(s["bc2_done"], 1)

            for n in range(4):
                spread_again(At(None, n))
            with pe.Fori(0, 14) as i:
                for q in range(4):
                    spread_again(At(i, 4 + q))
            for n in range(60, GROUPS):
                spread_again(At(None, n))

        @block.scalar
        def _(act):
            def high(g, k):
                if not g.exists():
                    return
                wait(act, s["xn_ready"], g.value(TILES, k + 1))
                before = g + -1
                wait(act, moved[before.slot(2)][k], before.round(2, 16 * COPIES, 16 * COPIES))
                nc.scalar.activation(inner(XH, k), square(XN[:, k, :]), ACT.Copy).then_inc(s["xh_ready"], 1)

            def gates(g, k, image):
                if not g.exists():
                    return
                wait(act, s["conv_done"], g.value(4, 2 * k + image + 1))
                wait(act, s["h_ready"], g.value(TILES, k - TILES + 1))
                to, a, b = rows_of(image), slice(0, CH), slice(CH, 128)
                nc.scalar.activation(F[to, k, :], conv[a, image, :], ACT.Sigmoid, bias=bias[a, :], scale=unscale[a, :])
                nc.scalar.activation(S[to, k, :], conv[b, image, :], ACT.Sigmoid, bias=bias[b, :], scale=unscale[b, :])
                nc.scalar.activation(Tc[to, k, :], conv[b, image, :], ACT.Identity, bias=bias_half[b, :],
                                     scale=unscale[b, :]).then_inc(s["evac_done"], 1)

            def squares(g, k):
                if not g.exists():
                    return
                wait(act, s["ym_ready"], g.value(TILES, k + 1))
                nc.scalar.activation(Y[:, k, :], Y[:, k, :], ACT.Square, accum_out=keep[:, g.slot(4), K_S2 + k:K_S2 + k + 1])\
                    .then_inc(s["sq_done"], 1)

            def step(g):
                gates(g + -1, 1, 1)
                high(g + 1, 0)
                high(g + 1, 1)
                gates(g, 0, 0)
                gates(g, 0, 1)
                squares(g + -2, 0)
                gates(g, 1, 0)
                squares(g + -2, 1)

            act.wait_ge(s["h0_in"], 64)
            for k in range(TILES):
                nc.scalar.activation(H[:, k, 0, :], H[:, k, 1, :], ACT.Sigmoid).then_inc(s["h_init"], 1)
            act.wait_ge(s["setup_done"], 1)
            for n in range(-1, 4):
                step(At(None, n))
            with act.Fori(0, 14) as i:
                for q in range(4):
                    step(At(i, 4 + q))
            for n in range(60, GROUPS + 2):
                step(At(None, n))

            act.wait_ge(s["coef_ready"], 1)

            def affine(g):
                for k in range(TILES):
                    slot = TILES * g.slot(XRING) + k
                    if k == 0:
                        wait(act, back_in[g.slot(XRING)], g.round(XRING, 128, 128))
                        wait(act, out_stored[g.slot(2)], (g + -2).round(2, 64, 64))
                    nc.scalar.activation(result(g, k), X[:, slot, :], ACT.Identity,
                                         scale=kept_of(g, k, coef_a), bias=kept_of(g, k, coef_b))\
                        .then_inc(s["w_done"], 1)

            for n in range(4):
                affine(At(None, n))
            with act.Fori(0, 14) as i:
                for q in range(4):
                    affine(At(i, 4 + q))
            for n in range(60, GROUPS):
                affine(At(None, n))

        @block.gpsimd
        def _(pool):
            nc.gpsimd.memset(power[:, :], -0.5)
            nc.gpsimd.memset(xscale[:, :], XSCALE)
            nc.gpsimd.memset(XH[:, :, :], 0.0)
            nc.gpsimd.memset(XL[:, :, :], 0.0)
            nc.gpsimd.memset(MK[:, :, :], 0.0).then_inc(s["zeroed"], 1)
            pool.wait_ge(s["zeroed"], 1)

            def low(g, k):
                if not g.exists():
                    return
                wait(pool, s["xh_ready"], g.value(TILES, k + 1))
                before = g + -1
                wait(pool, moved[before.slot(2)][k], before.round(2, 16 * COPIES, 16 * COPIES))
                nc.gpsimd.tensor_tensor(inner(XL, k), square(XN[:, k, :]), inner(XH, k), ALU.subtract)\
                    .then_inc(s["xl_ready"], 1)

            def add_h(g, k):
                if not g.exists():
                    return
                wait(pool, s["h_ready"], g.value(TILES, k + 1))
                at = X[:, TILES * g.slot(XRING) + k, :]
                nc.gpsimd.tensor_tensor(at, at, H[:, k, g.slot(2), :], ALU.add).then_inc(s["x1_ready"], 1)

            def rstd1(g):
                if not g.exists():
                    return
                wait(pool, s["ve1_ready"], g.value(1, 1))
                nc.gpsimd.tensor_tensor(pw1[:, :], ve1[:, :], power[:, :], ALU.pow).then_inc(s["pw1_done"], 1)
                wait(pool, s["pw1_done"], g.value(1, 1))
                nc.gpsimd.tensor_tensor(r1[:, :], pw1[:, :], xscale[:, :], ALU.mult)\
                    .then_inc(s["r1_ready"], 1)

            def rstd2(g):
                if not g.exists():
                    return
                wait(pool, s["ve2_ready"], g.value(1, 1))
                nc.gpsimd.tensor_tensor(keep[:, g.slot(4), K_RSTD:K_RSTD + TILES], ve2[:, :], power[:, :], ALU.pow).then_inc(s["r2_ready"], 1)

            def step(g):
                low(g + 1, 0)
                low(g + 1, 1)
                add_h(g + -1, 1)
                rstd2(g + -1)
                add_h(g, 0)
                rstd1(g + 2)

            for n in range(-2, 4):
                step(At(None, n))
            with pool.Fori(0, 14) as i:
                for q in range(4):
                    step(At(i, 4 + q))
            for n in range(60, GROUPS + 1):
                step(At(None, n))
            pool.wait_ge(s["pow_in"], 1)
            nc.gpsimd.tensor_tensor(end[:, 9:10], end[:, 8:9], power[:, 0:1], ALU.pow)\
                .then_inc(s["pow_out"], 1)

        @block.vector
        def _(dve):
            v = nc.vector
            prepared = [0]

            def then(ins):
                prepared[0] += 1
                ins.then_inc(s["prep"], 1)
                dve.wait_ge(s["prep"], prepared[0])

            v.memset(idle[:, :], 0.0)
            dve.wait_ge(s["consts_in"], 16)
            v.tensor_copy(ident16[:, :], consts[:, C_IDENT:C_IDENT + 128])
            then(v.tensor_copy(spread[:, :, :].rearrange("p a b -> p (a b)"), consts[:, C_SPREAD:C_SPREAD + 512]))
            taps = CH * TAPS
            dve.wait_ge(s["weights_in"], 96)
            w = X[:, 6, 0:taps]
            then(v.tensor_tensor(X[0:CH, 6, 0:taps], X[0:CH, 6, 0:taps], X[0:CH, 7, 0:taps], ALU.subtract))
            then(v.tensor_tensor(small[0:CH, 0:1], small[0:CH, 0:1], small[0:CH, 1:2], ALU.subtract))
            v.tensor_copy(bias[:, :], small[:, 0:1])
            then(v.tensor_scalar(bias_half[:, :], small[:, 0:1], 0.5, None, ALU.add))
            then(v.tensor_reduce(small[:, 2:3], w, AX, ALU.max, apply_absolute_value=True))
            then(v.tensor_scalar(small[:, 2:3], small[:, 2:3], 1e-30, 1e30, ALU.max, ALU.min))
            then(v.tensor_scalar(small[:, 3:4].bitcast(i32), small[:, 2:3].bitcast(i32), 0x7F800000, None,
                                 ALU.bitwise_and))
            v.tensor_scalar(unscale[:, :], small[:, 3:4], 1.0 / (WSCALE * XSCALE), None, ALU.mult)
            then(v.reciprocal(small[:, 7:8], small[:, 3:4]))
            then(v.tensor_scalar(w, w, small[:, 7:8], WSCALE, ALU.mult, ALU.mult))
            split = XN[:, 0, :].bitcast(f16)
            then(v.tensor_copy(split[:, 0:taps], w))
            v.tensor_tensor(split[:, 1024:1024 + taps], w, split[:, 0:taps], ALU.subtract).then_inc(s["split_ready"], 1)
            dve.wait_ge(s["transposed"], 1)
            for p in range(len(PASSES)):
                last = v.tensor_copy(wst[:, p, :], wprep(p))
            then(last)
            dve.wait_ge(s["zeroed"], 1)
            dve.wait_ge(s["h_init"], TILES)
            for k in range(TILES):
                last = v.scalar_tensor_tensor(H[:, k, 1, :], H[:, k, 1, :], 0.5, H[:, k, 0, :], ALU.add, ALU.max)
            then(last)
            v.tensor_copy(small[:, 8:9], small[:, 7:8]).then_inc(s["setup_done"], 1)

            def stats1(g):
                if not g.exists():
                    return
                dve.wait_ge(loaded[g.slot(XRING)], g.round(XRING, 64, 64))
                for k in range(TILES):
                    at = X[:, TILES * g.slot(XRING) + k, :]
                    v.bn_stats(bn1[:, k, 0:6], at[:, 0:HALF])
                    v.bn_stats(bn1[:, k, 6:12], at[:, HALF:PX]).then_inc(s["bn1_done"], 1)
                wait(dve, s["bn1_done"], g.value(TILES, TILES))
                v.tensor_copy(idle[:, 0:1], idle[:, 1:2])
                for k in range(TILES):
                    last = v.bn_aggr(mv1[:, k, :], bn1[:, k, :])
                last.then_inc(s["st1_ready"], 1)

            def stats2(g):
                if not g.exists():
                    return
                for k in range(TILES):
                    wait(dve, s["x1_ready"], g.value(TILES, k + 1))
                    at = X[:, TILES * g.slot(XRING) + k, :]
                    v.bn_stats(bn2[:, k, 0:6], at[:, 0:HALF])
                    v.bn_stats(bn2[:, k, 6:12], at[:, HALF:PX]).then_inc(s["bn2_done"], 1)
                wait(dve, s["bn2_done"], g.value(TILES, TILES))
                v.tensor_copy(idle[:, 0:1], idle[:, 1:2])
                for k in range(TILES):
                    last = v.bn_aggr(mv2[:, k, :], bn2[:, k, :])
                last.then_inc(s["st2_ready"], 1)

            def finish(g, at, mv, mean, dm, ve, averaged, link, ready):
                wait(dve, s[averaged], g.done(1))
                pair = stat[:, at:at + 4].rearrange("p (k m) -> p m k", m=2)
                v.tensor_copy(mean, pair[:, 0, :])
                v.tensor_tensor(dm[:, :], mv[:, :, 0], pair[:, 0, :], ALU.subtract).then_inc(s[link], 1)
                wait(dve, s[link], g.value(2, 1))
                v.tensor_tensor(dm[:, :], dm[:, :], dm[:, :], ALU.mult).then_inc(s[link], 1)
                wait(dve, s[link], g.value(2, 2))
                v.scalar_tensor_tensor(ve[:, :], dm[:, :], GN_EPS, pair[:, 1, :], ALU.add, ALU.add)\
                    .then_inc(s[ready], 1)

            def finish1(g):
                if not g.exists():
                    return
                wait(dve, s["r1_ready"], g.value(1, 0))
                finish(g, 0, mv1, mg1[:, :], dm1, ve1, "avg1_done", "link1", "ve1_ready")

            def finish2(g):
                if not g.exists():
                    return
                wait(dve, s["r2_ready"], g.value(1, 0))
                finish(g, 4, mv2, keep[:, g.slot(4), K_MEAN:K_MEAN + TILES], dm2, ve2, "avg2_done", "link2", "ve2_ready")

            def normalise1(g, k):
                if not g.exists():
                    return
                wait(dve, s["r1_ready"], g.done(1))
                wait(dve, s["xl_ready"], g.value(TILES, k - TILES + 1))
                v.tensor_scalar(XN[:, k, :], X[:, TILES * g.slot(XRING) + k, :], mg1[:, k:k + 1], r1[:, k:k + 1],
                                ALU.subtract, ALU.mult).then_inc(s["xn_ready"], 1)

            def recur(g, k):
                if not g.exists():
                    return
                wait(dve, s["evac_done"], g.value(4, 2 * k + 2))
                wait(dve, s["x1_ready"], g.value(TILES, k - 2 * TILES + 1))
                f, c, i = F[:, k, :], Tc[:, k, :], S[:, k, :]
                v.tensor_tensor(c, c, i, ALU.max).then_inc(s["g_ready"], 1)
                wait(dve, s["g_ready"], g.value(TILES, k + 1))
                v.scalar_tensor_tensor(i, f, 1.0, c, ALU.subtract, ALU.mult)
                v.tensor_tensor(f, f, H[:, k, (g + 1).slot(2), :], ALU.mult).then_inc(s["fh_ready"], 1)
                wait(dve, s["fh_ready"], g.value(TILES, k + 1))
                v.tensor_tensor(H[:, k, g.slot(2), :], f, i, ALU.subtract).then_inc(s["h_ready"], 1)

            def mask(g):
                if not g.exists():
                    return
                wait(dve, s["sums_done"], g.done(1))
                wait(dve, mask_out[g.slot(2)], (g + -2).round(2, 64, 64))
                v.tensor_scalar(MK[:, g.slot(2), :], sums[:, :], 0.0, None, ALU.not_equal, ALU.add,
                                accum_out=keep[:, g.slot(4), K_COUNT:K_COUNT + 1]).then_inc(s["mask_ready"], 1)

            def masked(g, k):
                if not g.exists():
                    return
                wait(dve, s["bc_done"], g.value(TILES, k + 1))
                v.scalar_tensor_tensor(Y[:, k, :], bcast[:, :], 1.0, Y[:, k, :], ALU.mult, ALU.mult,
                                       accum_out=keep[:, g.slot(4), K_S1 + k:K_S1 + k + 1]).then_inc(s["ym_ready"], 1)

            def store_kept(g):
                if not g.exists():
                    return
                wait(dve, s["sq_done"], g.done(TILES))
                wait(dve, s["ym_ready"], g.done(TILES))
                v.tensor_copy(kept_of(g), keep[:, g.slot(4), :])

            def normalise2(g):
                if not g.exists():
                    return
                wait(dve, s["r2_ready"], g.done(1))
                for k in range(TILES):
                    wait(dve, s["sq_done"], g.value(TILES, k - TILES + 1))
                    mean, rstd = (keep[:, g.slot(4), c + k:c + k + 1] for c in (K_MEAN, K_RSTD))
                    v.tensor_scalar(Y[:, k, :], X[:, TILES * g.slot(XRING) + k, :], mean, rstd,
                                    ALU.subtract, ALU.mult).then_inc(s["y_ready"], 1)
                wait(dve, s["y_ready"], g.done(TILES))
                v.tensor_copy(keep[:, g.slot(4), K_FIRST:K_FIRST + TILES], Y[:, :, 0])

            def step(g):
                normalise1(g + 1, 0)
                normalise1(g + 1, 1)
                recur(g + -1, 1)
                mask(g + -2)
                stats1(g + 2)
                stats2(g + -1)
                masked(g + -2, 0)
                finish2(g + -1)
                recur(g, 0)
                masked(g + -2, 1)
                store_kept(g + -3)
                finish1(g + 2)
                normalise2(g + -1)

            for n in range(-2, 4):
                step(At(None, n))
            with dve.Fori(0, 14) as i:
                for q in range(4):
                    step(At(i, 4 + q))
            for n in range(60, GROUPS + 3):
                step(At(None, n))

            v.tensor_copy(end[:, 0:1], kept[:, 0, 0:1]).then_inc(s["counts_ready"], 1)
            dve.wait_ge(s["counts_out"], 1)
            then(v.tensor_copy(counts[:, :, :].rearrange("p a b -> p (a b)"), stat[:, 0:7 * GROUPS]))
            then(v.reduce_max(end[:, 0:1], counts[:, 2:6, :].rearrange("p a b -> p (a b)"), AX))
            most = end[:, 0:1]
            v.tensor_scalar(first[:, :], counts[:, 6, :], most, consts[:, C_FIRST:C_FIRST + 1], ALU.is_lt, ALU.mult)
            then(v.tensor_scalar(padn[:, :, :], counts[:, 0:2, :].rearrange("p k g -> p g k"), most, -1.0,
                                 ALU.subtract, ALU.mult))
            y0 = kept[:, :, K_FIRST:K_FIRST + TILES]
            then(v.scalar_tensor_tensor(prod[:, :, :], padn[:, :, :], 1.0, y0, ALU.mult, ALU.mult,
                                        accum_out=end[:, 2:3]))
            then(v.scalar_tensor_tensor(padn[:, :, :], prod[:, :, :], 1.0, y0, ALU.mult, ALU.mult,
                                        accum_out=end[:, 3:4]))
            v.tensor_reduce(end[:, 4:5], kept[:, :, K_S1:K_S1 + TILES], mybir.AxisListType.XY, ALU.add)
            then(v.tensor_reduce(end[:, 5:6], kept[:, :, K_S2:K_S2 + TILES], mybir.AxisListType.XY, ALU.add))
            then(v.tensor_tensor(end[:, 4:6], end[:, 4:6], end[:, 2:4], ALU.add))
            v.tensor_copy(end[:, 1:2], end[:, 4:5]).then_inc(s["fold"], 1)
            then(v.tensor_scalar(end[:, 6:7], most, float(SEQS * STEPS), 1.0, ALU.mult, ALU.max))
            then(v.reciprocal(end[:, 7:8], end[:, 6:7]))
            dve.wait_ge(s["folded"], 1)
            then(v.tensor_scalar(end[:, 10:12], sums[:, 0:2], end[:, 7:8], None, ALU.mult))
            then(v.tensor_tensor(end[:, 7:8], end[:, 10:11], end[:, 10:11], ALU.mult))
            then(v.tensor_tensor(end[:, 8:9], end[:, 11:12], end[:, 7:8], ALU.subtract))
            then(v.tensor_scalar(end[:, 8:9], end[:, 8:9], 0.0, BN_EPS, ALU.max, ALU.add))
            v.tensor_copy(end[:, 1:2], end[:, 8:9]).then_inc(s["pow_in"], 1)
            mean, rstd = kept[:, :, K_MEAN:K_MEAN + TILES], kept[:, :, K_RSTD:K_RSTD + TILES]
            v.tensor_scalar(coef_a[:, :, :], rstd, 1.0, None, ALU.add)
            v.scalar_tensor_tensor(coef_b[:, :, :], rstd, -1.0, mean, ALU.mult, ALU.mult)
            dve.wait_ge(s["pow_out"], 1)
            then(v.tensor_scalar(end[:, 10:11], end[:, 9:10], -1.0, None, ALU.add))
            then(v.tensor_scalar(coef_c[:, :, :], rstd, end[:, 10:11], None, ALU.mult))
            v.tensor_copy(end[:, 1:2], end[:, 10:11]).then_inc(s["coef_ready"], 1)

            def fix_first(g):
                if not g.exists():
                    return
                wait(dve, back_in[g.slot(XRING)], g.round(XRING, 128, 128))
                at = MK[:, g.slot(XRING), 0:1]
                has_pad = first[:, g.plus:g.plus + 1] if g.i is None else first[:, bass.ds(g.value(1), 1)]
                v.tensor_tensor(at, at, has_pad, ALU.max).then_inc(s["first_fixed"], 1)

            def scale(g):
                for k in range(TILES):
                    wait(dve, s["bc2_done"], g.value(TILES, k + 1))
                    v.scalar_tensor_tensor(Tc[:, k, :], X[:, TILES * g.slot(XRING) + k, :], kept_of(g, K_MEAN + k),
                                           conv[:, k, :], ALU.subtract, ALU.mult).then_inc(s["t_done"], 1)
                for k in range(TILES):
                    wait(dve, s["t_done"], g.value(TILES, k + 1))
                    wait(dve, s["w_done"], g.value(TILES, k + 1))
                    at = result(g, k)
                    v.scalar_tensor_tensor(at, Tc[:, k, :], kept_of(g, k, coef_c), at, ALU.mult, ALU.add)\
                        .then_inc(s["out_ready"], 1)
                fix_first(g + 1)

            fix_first(At(None, 0))
            for n in range(4):
                scale(At(None, n))
            with dve.Fori(0, 14) as i:
                for q in range(4):
                    scale(At(i, 4 + q))
            for n in range(60, GROUPS):
                scale(At(None, n))


def kernel(**inputs):
    import numpy as np
    import concourse.bacc as bacc
    from concourse.bass_utils import run_bass_kernel_spmd

    nc = bacc.Bacc("TRN2", target_bir_lowering=False, num_devices=1)
    arrays, args = {}, []
    for name in ("x", "L0_conv_conv_w", "L0_conv_conv_b", "L0_conv_h0"):
        arrays["in_" + name] = np.ascontiguousarray(inputs[name])
    arrays["in_table"] = constant_table()
    for name, a in arrays.items():
        args.append(nc.dram_tensor(name, a.shape, mybir.dt.from_np(a.dtype), kind="ExternalInput").ap())
    out = nc.dram_tensor("out_dram", (SEQS * STEPS, CH, SIDE, SIDE), mybir.dt.float32, kind="ExternalOutput").ap()
    x1 = nc.dram_tensor("x1_dram", (SEQS, STEPS, CH, PX), mybir.dt.float32, kind="Internal").ap()
    masks = nc.dram_tensor("mask_dram", (4, GROUPS, 2, HALF), mybir.dt.bfloat16, kind="Internal").ap()
    preact_kernel(nc, *args, out, x1, masks)
    r = run_bass_kernel_spmd(nc, [arrays], core_ids=[0])
    return r.results[0]["out_dram"]
```

```python
import concourse.bass as bass
from concourse import mybir
from contextlib import ExitStack


SEQS, STEPS, CH, SIDE = 4, 64, 64, 32
PX = SIDE * SIDE
PAD = SIDE + 2
PP = PAD * PAD
HALF = PX // 2
ROWS = SIDE // 2
TAPS = 9
GROUPS = STEPS
TILES = 2
NT = GROUPS * TILES
XRING = 4
LAST = 4
RESIDENT = XRING + LAST
GN_EPS, BN_EPS = 1e-5, 1e-3
XSCALE = 512.0
WSCALE = 4096.0
COPIES = 6
PASSES = ([("parts", 0, t, t) for t in (4, 0, 1, 2, 3, 5, 6, 7, 8)] + [("rows", 1, t, t + 3) for t in range(3)]
          + [("columns", 1, 6, 7), ("parts", 1, 8, 8)])
K_S1, K_S2, K_MEAN, K_RSTD, K_FIRST, K_COUNT, K_END = 0, 2, 4, 6, 8, 10, 11

C_IDENT, C_SPREAD, C_PAIR, C_FOLD, C_OWN, C_ALL, C_ROW, C_SUM, C_FIRST, C_END = (
    0, 128, 640, 768, 896, 1152, 1664, 1792, 1824, 1825)
C_STAY = C_PAIR


def constant_table():
    import numpy as np

    t = np.zeros((128, C_END), np.float32)
    p = np.arange(128)
    t[:, C_IDENT:C_IDENT + 128] = p[:, None] == p[None]
    t[:, C_PAIR:C_PAIR + 128] = 0.5 * (p[:, None] // 2 == p[None] // 2)
    t[:, C_FOLD:C_FOLD + 128] = p[:, None] % CH == p[None] % CH
    for chunk in range(4):
        for image in range(2):
            row = 32 * chunk + 16 * image
            own = p // CH == image
            t[row, C_SPREAD + 128 * chunk:][:128] = own
            t[row, C_OWN + 128 * (chunk // 2):][:128] = own
            t[row, C_ALL + 128 * (2 * (chunk // 2) + image):][:128] = 1.0
            t[row, C_ROW + 64 * (chunk // 2) + 16 * image] = 1.0
            t[64 * (chunk // 2) + 16 * image, C_FIRST] = 1.0
    for image in range(2):
        t[image * CH:(image + 1) * CH, C_SUM + 16 * image] = 1.0
    return t


class At:

    def __init__(self, i, plus, times=4):
        self.i, self.plus, self.times = i, plus, times

    def __add__(self, n):
        return At(self.i, self.plus + n, self.times)

    def exists(self):
        return self.i is not None or 0 <= self.plus < GROUPS

    def value(self, each, more=0):
        known = each * self.plus + more
        return known if self.i is None else self.i * (each * self.times) + known

    def round(self, ring, each, more=0):
        known = each * (self.plus // ring) + more
        return known if self.i is None else self.i * (each * (self.times // ring)) + known

    def done(self, each):
        return self.value(each, each) if self.i is not None else each * min(self.plus + 1, GROUPS)

    def slot(self, ring):
        return self.plus % ring


def wait(engine, semaphore, value):
    if not isinstance(value, int) or value > 0:
        engine.wait_ge(semaphore, value)


def preact_kernel(nc, x, conv_w, conv_b, h0, table, out, x1_dram, mask_dram):
    f32, f16, bf16, i32 = mybir.dt.float32, mybir.dt.float16, mybir.dt.bfloat16, mybir.dt.int32
    ALU = mybir.AluOpType
    ACT = mybir.ActivationFunctionType
    AX = mybir.AxisListType.X

    x_v = x.rearrange("(b t) c h w -> b t c (h w)", b=SEQS)
    out_v = out.rearrange("(b t) c h w -> b t c (h w)", b=SEQS)
    h0_v = h0.rearrange("b c h w -> b c (h w)")
    w_v = conv_w.rearrange("o c h w -> o (c h w)")
    b_v = conv_b.rearrange("(g o a) -> g o a", g=3, a=1)

    ctx = ExitStack()
    with ctx:
        def sb(name, shape, dt=f32):
            return ctx.enter_context(nc.sbuf_tensor(name, shape, dt))

        def sem(name):
            return ctx.enter_context(nc.semaphore(name))

        staying = sb("staying", [128, C_END - C_STAY])
        spread = sb("spread", [128, 4, 128], bf16)
        ident16 = sb("ident16", [128, 128], f16)
        wst = sb("wst", [128, len(PASSES), 128], f16)
        bias = sb("bias", [128, 1])
        bias_half = sb("bias_half", [128, 1])
        unscale = sb("unscale", [128, 1])
        X = sb("X", [128, RESIDENT * TILES, PX])
        XN = sb("XN", [128, TILES, PX])
        XH = sb("XH", [128, TILES, PP], f16)
        XL = sb("XL", [128, TILES, PP], f16)
        U = sb("U", [128, 8, PP], f16)
        Z = sb("Z", [128, 8, SIDE * PAD], f16)
        V = sb("V", [128, 8, SIDE * PAD], f16)
        F = sb("F", [128, TILES, PX])
        S = sb("S", [128, TILES, PX])
        Tc = sb("Tc", [128, TILES, PX])
        H = sb("H", [128, TILES, PX])
        Y = sb("Y", [128, 2 * TILES, PX])
        MB = sb("MB", [128, TILES, PX], bf16)
        MK = sb("MK", [128, 4, HALF], bf16)
        bn1 = sb("bn1", [128, TILES, 12])
        bn2 = sb("bn2", [128, TILES, 12])
        mv = sb("mv", [128, 2 * TILES, 2])
        dm = sb("dm", [128, 2 * TILES])
        ve = sb("ve", [128, 2 * TILES])
        pw = sb("pw", [128, 2 * TILES])
        norm = sb("norm", [128, 2, 2 * TILES])
        power = sb("power", [128, 2 * TILES])
        scales = sb("scales", [128, 2 * TILES])
        idle = sb("idle", [128, 2])
        keep = sb("keep", [128, 4, K_END])
        kept = sb("kept", [128, GROUPS, K_END])
        small = sb("small", [128, 9])
        end = sb("end", [128, 12])
        counts = sb("counts", [128, 7, GROUPS])
        padn = sb("padn", [128, GROUPS, TILES])
        prod = sb("prod", [128, GROUPS, TILES])
        first = sb("first", [128, GROUPS])
        coef_a = sb("coef_a", [128, GROUPS, TILES])
        coef_b = sb("coef_b", [128, GROUPS, TILES])
        coef_c = sb("coef_c", [128, GROUPS, TILES])

        conv = ctx.enter_context(nc.psum_tensor("conv", [128, 2, PX], f32))
        sums = ctx.enter_context(nc.psum_tensor("sums", [128, HALF], f32))
        stat = ctx.enter_context(nc.psum_tensor("stat", [128, HALF], f32))

        names = """consts_in h0_in weights_in prep zeroed transposed split_ready h_init
            xn_ready xh_ready xl_ready conv_done evac_done g_ready fh_ready h_ready x1_ready
            bn1_done bn2_done pairs_ready pairs_done link ve_ready power_done
            r_ready y_ready sums_done mask_ready ym_ready sq_done stored
            counts_ready counts_out fold folded pow_in pow_out coef_ready
            spread_in weights_laid bc2_done t_done w_done first_fixed out_ready""".split()
        s = {n: sem(n) for n in names}
        loaded = [sem(f"loaded{n}") for n in range(XRING)]
        copied = [[sem(f"copied{p}{image}") for image in range(2)] for p in range(2)]
        mask_out = [sem(f"mask_out{p}") for p in range(2)]
        out_stored = [sem(f"out_stored{n}") for n in range(4)]
        masks_in = [sem(f"masks_in{n}") for n in range(XRING)]
        back_in = [sem(f"back_in{n}") for n in range(XRING)]

        def has_statistics(g):
            return (g + 2).exists() or (g + -1).exists()

        def wprep(p):
            return conv[:, 0, :].bitcast(f16)[:, 128 * p:128 * (p + 1)]

        def results(p):
            return (F[:, :, :], S[:, :, :], Y[:, 0:TILES, :], Y[:, TILES:2 * TILES, :])[p.slot(4)]

        def group_at(p):
            if p.i is not None or p.plus >= RESIDENT:
                return p + -RESIDENT
            return At(None, GROUPS - LAST + p.plus if p.plus < LAST else GROUPS - RESIDENT + p.plus - LAST)

        def x_slot(g):
            return XRING + g.plus - (GROUPS - LAST) if g.i is None and g.plus >= GROUPS - LAST else g.slot(XRING)

        def x_tile(g, k):
            return X[:, TILES * x_slot(g) + k, :]

        def step_of(v, g):
            if g.i is None:
                return v[g.plus]
            return v[bass.ds(g.value(1), 1)].rearrange("a c p -> (a c) p")

        def images_of(v, g, image):
            v = v[image::2]
            if g.i is None:
                return v[:, g.plus].rearrange("k c p -> c k p")
            return v[:, bass.ds(g.value(1), 1)].rearrange("k a c p -> (a c) k p")

        def operand_slot(g, image, k):
            return 4 * g.slot(2) + 2 * image + k

        def kept_of(g, column=None, t=kept):
            cols = slice(None) if column is None else slice(column, column + 1)
            if g.i is None:
                return t[:, g.plus, cols]
            return t[:, bass.ds(g.value(1), 1), cols].rearrange("p a b -> p (a b)")

        def group_of_x(g):
            slot = TILES * x_slot(g)
            return X[:, slot:slot + TILES, :].rearrange("p k x -> p (k x)")

        def mask_rows(slot):
            return MK[0:128:16, slot, :]

        const = lambda column, width: staying[:, column - C_STAY:column - C_STAY + width]
        once = X[:, TILES * (RESIDENT - 1) - 1, 0:C_STAY]
        WT = TILES * (RESIDENT - 1)
        inner = lambda t, k: t[:, k, :].rearrange("p (a b) -> p a b", b=PAD)[:, 1:1 + SIDE, 1:1 + SIDE]
        square = lambda ap: ap.rearrange("p (a b) -> p a b", b=SIDE)
        rows_of = lambda image: slice(CH * image, CH * (image + 1))

        block = ctx.enter_context(nc.Block())

        @block.sync
        def _(sp):

            def wait_all(*pairs):
                pairs = [(semaphore, v if isinstance(v, int) else sp.snap(sp.to_reg(v))) for semaphore, v in pairs]
                if any(not isinstance(value, int) for _, value in pairs):
                    sp.wait_ge(s["consts_in"], 16)
                for semaphore, value in pairs:
                    wait(sp, semaphore, value)

            def load(g):
                if not g.exists():
                    return
                if x_slot(g) < XRING:
                    wait_all((s["y_ready"], (g + -XRING).value(TILES, TILES)),
                             (s["stored"], (g + -XRING).value(16, 16)))
                slot = TILES * x_slot(g)
                for image in range(2):
                    sp.dma_start(X[rows_of(image), slot:slot + TILES, :], images_of(x_v, g, image))\
                        .then_inc(loaded[g.slot(XRING)], 16)

            def copies(g):
                if not g.exists():
                    return
                wait_all((s["xl_ready"], g.value(TILES, TILES)),
                         (s["conv_done"], (g + -2).value(4, 4)))
                n, used, below = SIDE * PAD, SIDE * PAD - 2, 2 * PAD
                for image in range(2):
                    done, slot = copied[g.slot(2)][image], operand_slot(g, image, 0)
                    both, of = slice(slot, slot + TILES), rows_of(image)
                    sp.dma_start(U[0:CH, both, :], XH[of, :, :]).then_inc(done, 16)
                    sp.dma_start(U[CH:128, both, :], XL[of, :, :]).then_inc(done, 16)
                    sp.dma_start(Z[0:CH, both, 0:n], XH[of, :, 0:n]).then_inc(done, 16)
                    sp.dma_start(Z[CH:128, both, 0:n], XH[of, :, PAD:PAD + n]).then_inc(done, 16)
                    sp.dma_start(V[0:CH, both, 0:used], XH[of, :, below:below + used]).then_inc(done, 16)
                    sp.dma_start(V[CH:128, both, 0:used], XH[of, :, below + 1:below + 1 + used]).then_inc(done, 16)

            def store(g):
                if not g.exists() or (g.i is None and g.plus >= GROUPS - RESIDENT):
                    return
                wait_all((s["x1_ready"], g.value(TILES, TILES)))
                sp.dma_start(step_of(x1_dram, g), group_of_x(g)).then_inc(s["stored"], 16)

            def store_mask(g):
                if not g.exists():
                    return
                wait_all((s["mask_ready"], g.value(1, 1)))
                sp.dma_start(step_of(mask_dram, g), mask_rows(g.slot(2))).then_inc(mask_out[g.slot(2)], 16)

            def spread_mask(g):
                if not g.exists():
                    return
                wait_all((mask_out[g.slot(2)], g.round(2, 16, 16)),
                         (s["ym_ready"], (g + -1).value(TILES, TILES)))
                rows = step_of(mask_dram, g).rearrange("(c i) x -> i c x", i=2)
                for image in range(2):
                    sp.dma_start(MB[rows_of(image), :, :].rearrange("p k x -> p (k x)")
                                 .rearrange("p (c x) -> p c x", x=HALF),
                                 rows[image:image + 1].broadcast_to([CH, 2 * TILES, HALF]))\
                        .then_inc(s["spread_in"], 16)

            def step(g):
                copies(g + 1)
                store_mask(g + -2)
                store(g + -1)
                load(g + 3)
                spread_mask(g + -2)

            load(At(None, 0))
            sp.dma_start(staying[:, :], table[:, C_STAY:]).then_inc(s["consts_in"], 16)
            taps = CH * TAPS
            sp.dma_start(once, table[:, 0:C_STAY]).then_inc(s["weights_in"], 16)
            sp.dma_start(X[0:CH, WT, 0:taps], w_v[0:CH, :]).then_inc(s["weights_in"], 16)
            sp.dma_start(X[0:CH, WT + 1, 0:taps], w_v[CH:2 * CH, :]).then_inc(s["weights_in"], 16)
            sp.dma_start(X[CH:128, WT, 0:taps], w_v[2 * CH:3 * CH, :]).then_inc(s["weights_in"], 16)
            sp.dma_start(small[0:CH, 0:1], b_v[0]).then_inc(s["weights_in"], 16)
            sp.dma_start(small[0:CH, 1:2], b_v[1]).then_inc(s["weights_in"], 16)
            sp.dma_start(small[CH:128, 0:1], b_v[2]).then_inc(s["weights_in"], 16)
            load(At(None, 1))
            for seq in range(SEQS):
                sp.dma_start(H[rows_of(seq % 2), seq // 2, :], h0_v[seq]).then_inc(s["h0_in"], 16)
            for n in range(-1, 4):
                step(At(None, n))
            with sp.Fori(0, 13) as i:
                for q in range(4):
                    step(At(i, 4 + q))
            for n in range(56, GROUPS + 2):
                step(At(None, n))

            sp.wait_ge(s["stored"], 16 * (GROUPS - RESIDENT))
            for p in range(2):
                sp.wait_ge(mask_out[p], 16 * (GROUPS // 2))

            def fetch(p):
                if not p.exists():
                    return
                before = (p + -XRING).value(TILES, TILES)
                wait_all((s["t_done"], before), (s["w_done"], before), (s["bc2_done"], before))
                g = group_at(p)
                sp.dma_start(mask_rows(p.slot(XRING)), step_of(mask_dram, g)).then_inc(masks_in[p.slot(XRING)], 16)
                if p.i is not None or p.plus >= RESIDENT:
                    sp.dma_start(group_of_x(g), step_of(x1_dram, g)).then_inc(back_in[p.slot(XRING)], 16)

            def put(p):
                wait_all((s["out_ready"], p.value(TILES, TILES)))
                for image in range(2):
                    sp.dma_start(images_of(out_v, group_at(p), image), results(p)[rows_of(image)])\
                        .then_inc(out_stored[p.slot(4)], 16)

            for n in range(3):
                fetch(At(None, n))
            for n in range(8):
                fetch(At(None, n + 3))
                put(At(None, n))
            with sp.Fori(0, 13) as i:
                for q in range(4):
                    fetch(At(i, 11 + q))
                    put(At(i, 8 + q))
            for n in range(60, GROUPS):
                fetch(At(None, n + 3))
                put(At(None, n))
            for stored in out_stored:
                sp.wait_ge(stored, 32 * (GROUPS // 4))

        @block.tensor
        def _(pe):
            mm = nc.tensor.matmul
            pe.wait_ge(s["consts_in"], 16)

            def unit(g, k, image):
                if not g.exists():
                    return
                if k == 0:
                    wait(pe, copied[g.slot(2)][image], g.round(2, 16 * COPIES, 16 * COPIES))
                wait(pe, s["evac_done"], g.value(4, 2 * k + image - 1))
                slot = operand_slot(g, image, k)
                for p, (operand, _, tap, other) in enumerate(PASSES):
                    (ky, kx), (ky2, kx2) = divmod(tap, 3), divmod(other, 3)
                    above = 2 if operand == "columns" else 0
                    padded = dict(parts=U, rows=Z, columns=V)[operand][:, slot, :].rearrange("p (a b) -> p a b", b=PAD)
                    left, right = int(kx == kx2 == 0), SIDE - int(kx == kx2 == 2)
                    for h in range(2):
                        top, bottom = h * ROWS, (h + 1) * ROWS
                        if h == 0 and ky == ky2 == 0:
                            top += 1
                        if h == 1 and ky == ky2 == 2:
                            bottom -= 1
                        last = mm(square(conv[:, image, :])[:, top:bottom, left:right], wst[:, p, :],
                                  padded[:, top + ky - above:bottom + ky - above, left + kx:right + kx],
                                  start=(p == 0), stop=(p == len(PASSES) - 1))
                last.then_inc(s["conv_done"], 1)

            def average(g):
                if not has_statistics(g):
                    return
                wait(pe, s["pairs_ready"], g.value(1, 3))
                wait(pe, s["ve_ready"], g.value(1, 2))
                mm(stat[:, 0:4 * TILES], const(C_PAIR, 128), mv[:, :, :].rearrange("p k m -> p (k m)"),
                   start=True, stop=True).then_inc(s["pairs_done"], 1)

            def channel_sums(g):
                if not g.exists():
                    return
                wait(pe, s["y_ready"], g.value(TILES, TILES))
                wait(pe, s["mask_ready"], g.value(1, 0))
                for chunk in range(4):
                    k, h = divmod(chunk, 2)
                    last = mm(sums[32 * chunk:32 * chunk + 32, :], const(C_SUM, 32),
                              Y[:, TILES * g.slot(2) + k, h * HALF:(h + 1) * HALF], start=True, stop=True)
                last.then_inc(s["sums_done"], 1)

            def step(g):
                unit(g, 0, 0)
                channel_sums(g + -2)
                unit(g, 0, 1)
                unit(g, 1, 0)
                average(g)
                unit(g, 1, 1)

            step(At(None, -2))
            step(At(None, -1))
            pe.wait_ge(s["split_ready"], 1)
            split = Tc[:, 0, :].bitcast(f16)
            for p, (_, low, first_tap, next_tap) in enumerate(PASSES):
                part = split[:, low * 1024:low * 1024 + CH * TAPS].rearrange("p (c t) -> p t c", t=TAPS)
                for n, tap in enumerate((first_tap, next_tap)):
                    last = nc.tensor.transpose(wprep(p)[CH * n:CH * (n + 1), :], part[:, tap, :], ident16[:, :])
            last.then_inc(s["transposed"], 1)
            pe.wait_ge(s["weights_laid"], 1)
            for n in range(4):
                step(At(None, n))
            with pe.Fori(0, 13) as i:
                for q in range(4):
                    step(At(i, 4 + q))
            for n in range(56, GROUPS + 2):
                step(At(None, n))

            pe.wait_ge(s["counts_ready"], 1)
            for n in range(6):
                mm(stat[:, GROUPS * n:GROUPS * (n + 1)], const(C_OWN + 128 * n, 128),
                   kept[:, :, K_COUNT], start=True, stop=True)
            mm(stat[:, GROUPS * 6:GROUPS * 7], const(C_ROW, 128), kept[:, :, K_COUNT],
               start=True, stop=True).then_inc(s["counts_out"], 1)
            pe.wait_ge(s["fold"], 1)
            mm(sums[:, 0:2], const(C_FOLD, 128), end[:, 4:6], start=True, stop=True)\
                .then_inc(s["folded"], 1)

            def spread_again(p):
                for k in range(TILES):
                    if k == 0:
                        wait(pe, s["first_fixed"], p.value(1, 1))
                    wait(pe, s["t_done"], p.value(TILES, k - 1))
                    for h in range(2):
                        last = mm(conv[:, k, h * HALF:(h + 1) * HALF], spread[:, 2 * k + h, :],
                                  MK[:, p.slot(XRING), :], start=True, stop=True)
                    last.then_inc(s["bc2_done"], 1)

            for n in range(8):
                spread_again(At(None, n))
            with pe.Fori(0, 14) as i:
                for q in range(4):
                    spread_again(At(i, 8 + q))

        @block.scalar
        def _(act):
            def high(g, k):
                if not g.exists():
                    return
                wait(act, s["xn_ready"], g.value(TILES, k + 1))
                before = g + -1
                for image in range(2):
                    wait(act, copied[before.slot(2)][image], before.round(2, 16 * COPIES, 16 * COPIES))
                nc.scalar.activation(inner(XH, k), square(XN[:, k, :]), ACT.Copy).then_inc(s["xh_ready"], 1)

            def gates(g, k, image):
                if not g.exists():
                    return
                wait(act, s["conv_done"], g.value(4, 2 * k + image + 1))
                wait(act, s["h_ready"], g.value(TILES, k - TILES + 1))
                to, a, b = rows_of(image), slice(0, CH), slice(CH, 128)
                nc.scalar.activation(F[to, k, :], conv[a, image, :], ACT.Sigmoid, bias=bias[a, :], scale=unscale[a, :])
                nc.scalar.activation(S[to, k, :], conv[b, image, :], ACT.Sigmoid, bias=bias[b, :], scale=unscale[b, :])
                nc.scalar.activation(Tc[to, k, :], conv[b, image, :], ACT.Identity, bias=bias_half[b, :],
                                     scale=unscale[b, :]).then_inc(s["evac_done"], 1)

            def squares(g, k):
                if not g.exists():
                    return
                wait(act, s["ym_ready"], g.value(TILES, k + 1))
                at = Y[:, TILES * g.slot(2) + k, :]
                nc.scalar.activation(at, at, ACT.Square, accum_out=keep[:, g.slot(4), K_S2 + k:K_S2 + k + 1])\
                    .then_inc(s["sq_done"], 1)

            def step(g):
                gates(g + -1, 1, 1)
                high(g + 1, 0)
                high(g + 1, 1)
                gates(g, 0, 0)
                gates(g, 0, 1)
                squares(g + -3, 0)
                gates(g, 1, 0)
                squares(g + -3, 1)

            act.wait_ge(s["h0_in"], 64)
            for k in range(TILES):
                nc.scalar.activation(S[:, k, :], H[:, k, :], ACT.Sigmoid).then_inc(s["h_init"], 1)
            act.wait_ge(s["zeroed"], 1)
            for n in range(-1, 4):
                step(At(None, n))
            with act.Fori(0, 13) as i:
                for q in range(4):
                    step(At(i, 4 + q))
            for n in range(56, GROUPS + 3):
                step(At(None, n))

            act.wait_ge(s["coef_ready"], 1)

            def affine(p):
                g = group_at(p)
                for k in range(TILES):
                    if k == 0 and (p.i is not None or p.plus >= RESIDENT):
                        wait(act, back_in[p.slot(XRING)], (p + -RESIDENT).round(XRING, 16, 16))
                    if k == 0:
                        wait(act, out_stored[p.slot(4)], (p + -4).round(4, 32, 32))
                    nc.scalar.activation(results(p)[:, k, :], x_tile(g, k), ACT.Identity,
                                         scale=kept_of(g, k, coef_a), bias=kept_of(g, k, coef_b))\
                        .then_inc(s["w_done"], 1)

            for n in range(8):
                affine(At(None, n))
            with act.Fori(0, 14) as i:
                for q in range(4):
                    affine(At(i, 8 + q))

        @block.gpsimd
        def _(pool):
            nc.gpsimd.memset(power[:, :], -0.5)
            nc.gpsimd.memset(scales[:, 0:TILES], XSCALE)
            nc.gpsimd.memset(scales[:, TILES:2 * TILES], 1.0)
            nc.gpsimd.memset(mv[:, :, :], 0.0)
            nc.gpsimd.memset(XH[:, :, :], 0.0)
            nc.gpsimd.memset(XL[:, :, :], 0.0)
            nc.gpsimd.memset(MK[:, :, :], 0.0).then_inc(s["zeroed"], 1)
            pool.wait_ge(s["zeroed"], 1)

            def low(g, k):
                if not g.exists():
                    return
                wait(pool, s["xh_ready"], g.value(TILES, k + 1))
                before = g + -1
                for image in range(2):
                    wait(pool, copied[before.slot(2)][image], before.round(2, 16 * COPIES, 16 * COPIES))
                nc.gpsimd.tensor_tensor(inner(XL, k), square(XN[:, k, :]), inner(XH, k), ALU.subtract)\
                    .then_inc(s["xl_ready"], 1)

            def add_h(g, k):
                if not g.exists():
                    return
                wait(pool, s["h_ready"], g.value(TILES, k + 1))
                at = x_tile(g, k)
                nc.gpsimd.tensor_tensor(at, at, H[:, k, :], ALU.add).then_inc(s["x1_ready"], 1)

            def rstd(g):
                if not has_statistics(g):
                    return
                wait(pool, s["ve_ready"], g.value(1, 3))
                nc.gpsimd.tensor_tensor(pw[:, :], ve[:, :], power[:, :], ALU.pow).then_inc(s["power_done"], 1)
                wait(pool, s["power_done"], g.value(1, 3))
                nc.gpsimd.tensor_tensor(norm[:, 1, :], pw[:, :], scales[:, :], ALU.mult).then_inc(s["r_ready"], 1)

            def step(g):
                low(g + 1, 0)
                low(g + 1, 1)
                add_h(g + -1, 1)
                rstd(g)
                add_h(g, 0)

            for n in range(-2, 4):
                step(At(None, n))
            with pool.Fori(0, 13) as i:
                for q in range(4):
                    step(At(i, 4 + q))
            for n in range(56, GROUPS + 1):
                step(At(None, n))
            pool.wait_ge(s["pow_in"], 1)
            nc.gpsimd.tensor_tensor(end[:, 9:10], end[:, 8:9], power[:, 0:1], ALU.pow)\
                .then_inc(s["pow_out"], 1)

        @block.vector
        def _(dve):
            v = nc.vector
            prepared = [0]

            def then(ins):
                prepared[0] += 1
                ins.then_inc(s["prep"], 1)
                dve.wait_ge(s["prep"], prepared[0])

            v.memset(idle[:, :], 0.0)
            dve.wait_ge(s["consts_in"], 16)

            def stats1(g):
                if not g.exists():
                    return
                dve.wait_ge(loaded[g.slot(XRING)], g.round(XRING, 32, 32))
                for k in range(TILES):
                    at = x_tile(g, k)
                    v.bn_stats(bn1[:, k, 0:6], at[:, 0:HALF])
                    v.bn_stats(bn1[:, k, 6:12], at[:, HALF:PX]).then_inc(s["bn1_done"], 1)
                wait(dve, s["bn1_done"], g.value(TILES, TILES))
                v.tensor_copy(idle[:, 0:1], idle[:, 1:2])
                for k in range(TILES):
                    last = v.bn_aggr(mv[:, k, :], bn1[:, k, :])
                return last

            def stats2(g):
                if not g.exists():
                    return
                for k in range(TILES):
                    wait(dve, s["x1_ready"], g.value(TILES, k + 1))
                    at = x_tile(g, k)
                    v.bn_stats(bn2[:, k, 0:6], at[:, 0:HALF])
                    v.bn_stats(bn2[:, k, 6:12], at[:, HALF:PX]).then_inc(s["bn2_done"], 1)
                wait(dve, s["bn2_done"], g.value(TILES, TILES))
                v.tensor_copy(idle[:, 0:1], idle[:, 1:2])
                for k in range(TILES):
                    last = v.bn_aggr(mv[:, TILES + k, :], bn2[:, k, :])
                return last

            def statistics(g):
                made = [stats1(g + 2), stats2(g + -1)]
                if has_statistics(g):
                    (made[1] or made[0]).then_inc(s["pairs_ready"], 1)

            def finish(g):
                if not has_statistics(g):
                    return
                wait(dve, s["pairs_done"], g.value(1, 3))
                wait(dve, s["r_ready"], g.value(1, 2))
                pair = stat[:, 0:4 * TILES].rearrange("p (k m) -> p m k", m=2)
                v.tensor_copy(norm[:, 0, :], pair[:, 0, :])
                v.tensor_tensor(dm[:, :], mv[:, :, 0], pair[:, 0, :], ALU.subtract).then_inc(s["link"], 1)
                wait(dve, s["link"], g.value(2, 5))
                v.tensor_tensor(dm[:, :], dm[:, :], dm[:, :], ALU.mult).then_inc(s["link"], 1)
                wait(dve, s["link"], g.value(2, 6))
                v.scalar_tensor_tensor(ve[:, :], dm[:, :], GN_EPS, pair[:, 1, :], ALU.add, ALU.add)\
                    .then_inc(s["ve_ready"], 1)

            def normalise1(g, k):
                if not g.exists():
                    return
                wait(dve, s["r_ready"], g.value(1, 1))
                wait(dve, s["xl_ready"], g.value(TILES, k - TILES + 1))
                v.tensor_scalar(XN[:, k, :], x_tile(g, k), norm[:, 0, k:k + 1], norm[:, 1, k:k + 1],
                                ALU.subtract, ALU.mult).then_inc(s["xn_ready"], 1)

            def recur(g, k):
                if not g.exists():
                    return
                wait(dve, s["evac_done"], g.value(4, 2 * k + 2))
                wait(dve, s["x1_ready"], g.value(TILES, k - TILES + 1))
                f, c, i = F[:, k, :], Tc[:, k, :], S[:, k, :]
                v.tensor_tensor(c, c, i, ALU.max).then_inc(s["g_ready"], 1)
                wait(dve, s["g_ready"], g.value(TILES, k + 1))
                v.scalar_tensor_tensor(i, f, 1.0, c, ALU.subtract, ALU.mult)
                v.tensor_tensor(f, f, H[:, k, :], ALU.mult).then_inc(s["fh_ready"], 1)
                wait(dve, s["fh_ready"], g.value(TILES, k + 1))
                v.tensor_tensor(H[:, k, :], f, i, ALU.subtract).then_inc(s["h_ready"], 1)

            def mask(g):
                if not g.exists():
                    return
                wait(dve, s["sums_done"], g.done(1))
                wait(dve, mask_out[g.slot(2)], (g + -2).round(2, 16, 16))
                v.tensor_scalar(MK[:, g.slot(2), :], sums[:, :], 0.0, None, ALU.not_equal, ALU.add,
                                accum_out=keep[:, g.slot(4), K_COUNT:K_COUNT + 1]).then_inc(s["mask_ready"], 1)

            def masked(g, k):
                if not g.exists():
                    return
                wait(dve, s["spread_in"], g.value(32, 32))
                at = Y[:, TILES * g.slot(2) + k, :]
                v.scalar_tensor_tensor(at, MB[:, k, :], 1.0, at, ALU.mult, ALU.mult,
                                       accum_out=keep[:, g.slot(4), K_S1 + k:K_S1 + k + 1]).then_inc(s["ym_ready"], 1)

            def store_kept(g):
                if not g.exists():
                    return
                wait(dve, s["sq_done"], g.done(TILES))
                wait(dve, s["ym_ready"], g.done(TILES))
                v.tensor_copy(kept_of(g), keep[:, g.slot(4), :])

            def normalise2(g):
                if not g.exists():
                    return
                wait(dve, s["r_ready"], g.value(1, 4))
                Yg = Y[:, TILES * g.slot(2):TILES * g.slot(2) + TILES, :]
                for k in range(TILES):
                    wait(dve, s["sq_done"], (g + -2).value(TILES, k + 1))
                    mean, rstd = (norm[:, n, TILES + k:TILES + k + 1] for n in range(2))
                    v.tensor_scalar(Yg[:, k, :], x_tile(g, k), mean, rstd,
                                    ALU.subtract, ALU.mult).then_inc(s["y_ready"], 1)
                v.tensor_copy(keep[:, g.slot(4), K_MEAN:K_RSTD + TILES].rearrange("p (n k) -> p n k", n=2),
                              norm[:, :, TILES:2 * TILES])
                wait(dve, s["y_ready"], g.done(TILES))
                v.tensor_copy(keep[:, g.slot(4), K_FIRST:K_FIRST + TILES], Yg[:, :, 0])

            def step(g):
                normalise1(g + 1, 0)
                normalise1(g + 1, 1)
                recur(g + -1, 1)
                mask(g + -2)
                statistics(g)
                masked(g + -3, 0)
                recur(g, 0)
                finish(g)
                masked(g + -3, 1)
                store_kept(g + -4)
                normalise2(g + -1)

            dve.wait_ge(s["zeroed"], 1)
            step(At(None, -2))
            taps = CH * TAPS
            dve.wait_ge(s["weights_in"], 112)
            v.tensor_copy(ident16[:, :], once[:, C_IDENT:C_IDENT + 128])
            then(v.tensor_copy(spread[:, :, :].rearrange("p a b -> p (a b)"), once[:, C_SPREAD:C_SPREAD + 512]))
            w = X[:, WT, 0:taps]
            then(v.tensor_tensor(X[0:CH, WT, 0:taps], X[0:CH, WT, 0:taps], X[0:CH, WT + 1, 0:taps], ALU.subtract))
            then(v.tensor_tensor(small[0:CH, 0:1], small[0:CH, 0:1], small[0:CH, 1:2], ALU.subtract))
            step(At(None, -1))
            v.tensor_copy(bias[:, :], small[:, 0:1])
            then(v.tensor_scalar(bias_half[:, :], small[:, 0:1], 0.5, None, ALU.add))
            then(v.tensor_reduce(small[:, 2:3], w, AX, ALU.max, apply_absolute_value=True))
            then(v.tensor_scalar(small[:, 2:3], small[:, 2:3], 1e-30, 1e30, ALU.max, ALU.min))
            then(v.tensor_scalar(small[:, 3:4].bitcast(i32), small[:, 2:3].bitcast(i32), 0x7F800000, None,
                                 ALU.bitwise_and))
            v.tensor_scalar(unscale[:, :], small[:, 3:4], 1.0 / (WSCALE * XSCALE), None, ALU.mult)
            then(v.reciprocal(small[:, 7:8], small[:, 3:4]))
            then(v.tensor_scalar(w, w, small[:, 7:8], WSCALE, ALU.mult, ALU.mult))
            split = Tc[:, 0, :].bitcast(f16)
            then(v.tensor_copy(split[:, 0:taps], w))
            v.tensor_tensor(split[:, 1024:1024 + taps], w, split[:, 0:taps], ALU.subtract).then_inc(s["split_ready"], 1)
            dve.wait_ge(s["transposed"], 1)
            for p in range(len(PASSES)):
                last = v.tensor_copy(wst[:, p, :], wprep(p))
            last.then_inc(s["weights_laid"], 1)
            dve.wait_ge(s["h_init"], TILES)
            for k in range(TILES):
                last = v.scalar_tensor_tensor(H[:, k, :], H[:, k, :], 0.5, S[:, k, :], ALU.add, ALU.max)
            then(last)
            for n in range(4):
                step(At(None, n))
            with dve.Fori(0, 13) as i:
                for q in range(4):
                    step(At(i, 4 + q))
            for n in range(56, GROUPS + 4):
                step(At(None, n))

            v.tensor_copy(end[:, 0:1], kept[:, 0, 0:1]).then_inc(s["counts_ready"], 1)
            dve.wait_ge(s["counts_out"], 1)
            then(v.tensor_copy(counts[:, :, :].rearrange("p a b -> p (a b)"), stat[:, 0:7 * GROUPS]))
            then(v.reduce_max(end[:, 0:1], counts[:, 2:6, :].rearrange("p a b -> p (a b)"), AX))
            most = end[:, 0:1]
            v.tensor_scalar(first[:, :], counts[:, 6, :], most, const(C_FIRST, 1), ALU.is_lt, ALU.mult)
            then(v.tensor_scalar(padn[:, :, :], counts[:, 0:2, :].rearrange("p k g -> p g k"), most, -1.0,
                                 ALU.subtract, ALU.mult))
            y0 = kept[:, :, K_FIRST:K_FIRST + TILES]
            then(v.scalar_tensor_tensor(prod[:, :, :], padn[:, :, :], 1.0, y0, ALU.mult, ALU.mult,
                                        accum_out=end[:, 2:3]))
            then(v.scalar_tensor_tensor(padn[:, :, :], prod[:, :, :], 1.0, y0, ALU.mult, ALU.mult,
                                        accum_out=end[:, 3:4]))
            v.tensor_reduce(end[:, 4:5], kept[:, :, K_S1:K_S1 + TILES], mybir.AxisListType.XY, ALU.add)
            then(v.tensor_reduce(end[:, 5:6], kept[:, :, K_S2:K_S2 + TILES], mybir.AxisListType.XY, ALU.add))
            then(v.tensor_tensor(end[:, 4:6], end[:, 4:6], end[:, 2:4], ALU.add))
            v.tensor_copy(end[:, 1:2], end[:, 4:5]).then_inc(s["fold"], 1)
            then(v.tensor_scalar(end[:, 6:7], most, float(SEQS * STEPS), 1.0, ALU.mult, ALU.max))
            then(v.reciprocal(end[:, 7:8], end[:, 6:7]))
            dve.wait_ge(s["folded"], 1)
            then(v.tensor_scalar(end[:, 10:12], sums[:, 0:2], end[:, 7:8], None, ALU.mult))
            then(v.tensor_tensor(end[:, 7:8], end[:, 10:11], end[:, 10:11], ALU.mult))
            then(v.tensor_tensor(end[:, 8:9], end[:, 11:12], end[:, 7:8], ALU.subtract))
            then(v.tensor_scalar(end[:, 8:9], end[:, 8:9], 0.0, BN_EPS, ALU.max, ALU.add))
            v.tensor_copy(end[:, 1:2], end[:, 8:9]).then_inc(s["pow_in"], 1)
            mean, rstd = kept[:, :, K_MEAN:K_MEAN + TILES], kept[:, :, K_RSTD:K_RSTD + TILES]
            v.tensor_scalar(coef_a[:, :, :], rstd, 1.0, None, ALU.add)
            v.scalar_tensor_tensor(coef_b[:, :, :], rstd, -1.0, mean, ALU.mult, ALU.mult)
            dve.wait_ge(s["pow_out"], 1)
            then(v.tensor_scalar(end[:, 10:11], end[:, 9:10], -1.0, None, ALU.add))
            then(v.tensor_scalar(coef_c[:, :, :], rstd, end[:, 10:11], None, ALU.mult))
            v.tensor_copy(end[:, 1:2], end[:, 10:11]).then_inc(s["coef_ready"], 1)

            def fix_first(p):
                if not p.exists():
                    return
                wait(dve, masks_in[p.slot(XRING)], p.round(XRING, 16, 16))
                at, g = MK[:, p.slot(XRING), 0:1], group_at(p)
                has_pad = first[:, g.plus:g.plus + 1] if g.i is None else first[:, bass.ds(g.value(1), 1)]
                v.tensor_tensor(at, at, has_pad, ALU.max).then_inc(s["first_fixed"], 1)

            def scale(p):
                g = group_at(p)
                fix_first(p + 1)
                for k in range(TILES):
                    wait(dve, s["bc2_done"], p.value(TILES, k + 1))
                    wait(dve, s["out_ready"], p.value(TILES, k - 1))
                    if k == 0 and (p.i is not None or p.plus >= RESIDENT):
                        wait(dve, back_in[p.slot(XRING)], (p + -RESIDENT).round(XRING, 16, 16))
                    v.scalar_tensor_tensor(Tc[:, k, :], x_tile(g, k), kept_of(g, K_MEAN + k),
                                           conv[:, k, :], ALU.subtract, ALU.mult).then_inc(s["t_done"], 1)
                for k in range(TILES):
                    wait(dve, s["t_done"], p.value(TILES, k + 1))
                    wait(dve, s["w_done"], p.value(TILES, k + 1))
                    at = results(p)[:, k, :]
                    v.scalar_tensor_tensor(at, Tc[:, k, :], kept_of(g, k, coef_c), at, ALU.mult, ALU.add)\
                        .then_inc(s["out_ready"], 1)

            fix_first(At(None, 0))
            for n in range(8):
                scale(At(None, n))
            with dve.Fori(0, 13) as i:
                for q in range(4):
                    scale(At(i, 8 + q))
            for n in range(60, GROUPS):
                scale(At(None, n))


def kernel(**inputs):
    import numpy as np
    import concourse.bacc as bacc
    from concourse.bass_utils import run_bass_kernel_spmd

    nc = bacc.Bacc("TRN2", target_bir_lowering=False, num_devices=1)
    arrays, args = {}, []
    for name in ("x", "L0_conv_conv_w", "L0_conv_conv_b", "L0_conv_h0"):
        arrays["in_" + name] = np.ascontiguousarray(inputs[name])
    arrays["in_table"] = constant_table()
    for name, a in arrays.items():
        args.append(nc.dram_tensor(name, a.shape, mybir.dt.from_np(a.dtype), kind="ExternalInput").ap())
    out = nc.dram_tensor("out_dram", (SEQS * STEPS, CH, SIDE, SIDE), mybir.dt.float32, kind="ExternalOutput").ap()
    x1 = nc.dram_tensor("x1_dram", (GROUPS - RESIDENT, 128, TILES * PX), mybir.dt.float32, kind="Internal").ap()
    masks = nc.dram_tensor("mask_dram", (GROUPS, 8, HALF), mybir.dt.bfloat16, kind="Internal").ap()
    preact_kernel(nc, *args, out, x1, masks)
    r = run_bass_kernel_spmd(nc, [arrays], core_ids=[0])
    return r.results[0]["out_dram"]
```

```python
import concourse.bass as bass
from concourse import mybir
from contextlib import ExitStack


SEQS, STEPS, CH, SIDE = 4, 64, 64, 32
PX = SIDE * SIDE
PAD = SIDE + 2
PP = PAD * PAD
HALF = PX // 2
ROWS = SIDE // 2
TAPS = 9
GROUPS = STEPS
TILES = 2
NT = GROUPS * TILES
UNROLL = 4
LOOP_END = GROUPS - 2 * UNROLL
LOOPS = LOOP_END // UNROLL - 1
XRING = 4
LAST = 4
RESIDENT = XRING + LAST
EARLY = 10
LATER = RESIDENT + EARLY
GN_EPS, BN_EPS = 1e-5, 1e-3
XSCALE = 512.0
WSCALE = 4096.0
COPIES = 6
PASSES = ([("parts", 0, t, t) for t in (4, 0, 1, 2, 3, 5, 6, 7, 8)] + [("rows", 1, t, t + 3) for t in range(3)]
          + [("columns", 1, 6, 7), ("parts", 1, 8, 8)])
K_S1, K_S2, K_MEAN, K_RSTD, K_FIRST, K_COUNT, K_END = 0, 2, 4, 6, 8, 10, 11

C_IDENT, C_SPREAD, C_PAIR, C_FOLD, C_OWN, C_ALL, C_ROW, C_SUM, C_FIRST, C_END = (
    0, 128, 640, 768, 896, 1152, 1664, 1792, 1824, 1825)
C_STAY = C_PAIR


def constant_table():
    import numpy as np

    t = np.zeros((128, C_END), np.float32)
    p = np.arange(128)
    t[:, C_IDENT:C_IDENT + 128] = p[:, None] == p[None]
    t[:, C_PAIR:C_PAIR + 128] = 0.5 * (p[:, None] // 2 == p[None] // 2)
    t[:, C_FOLD:C_FOLD + 128] = p[:, None] % CH == p[None] % CH
    for chunk in range(4):
        for image in range(2):
            row = 32 * chunk + 16 * image
            own = p // CH == image
            t[row, C_SPREAD + 128 * chunk:][:128] = own
            t[row, C_OWN + 128 * (chunk // 2):][:128] = own
            t[row, C_ALL + 128 * (2 * (chunk // 2) + image):][:128] = 1.0
            t[row, C_ROW + 64 * (chunk // 2) + 16 * image] = 1.0
            t[64 * (chunk // 2) + 16 * image, C_FIRST] = 1.0
    for image in range(2):
        t[image * CH:(image + 1) * CH, C_SUM + 16 * image] = 1.0
    return t


class At:

    def __init__(self, i, plus, times=4):
        self.i, self.plus, self.times = i, plus, times

    def __add__(self, n):
        return At(self.i, self.plus + n, self.times)

    def exists(self):
        return self.i is not None or 0 <= self.plus < GROUPS

    def value(self, each, more=0):
        known = each * self.plus + more
        return known if self.i is None else self.i * (each * self.times) + known

    def round(self, ring, each, more=0):
        known = each * (self.plus // ring) + more
        return known if self.i is None else self.i * (each * (self.times // ring)) + known

    def done(self, each):
        return self.value(each, each) if self.i is not None else each * min(self.plus + 1, GROUPS)

    def slot(self, ring):
        return self.plus % ring


def wait(engine, semaphore, value):
    if not isinstance(value, int) or value > 0:
        engine.wait_ge(semaphore, value)


def preact_kernel(nc, x, conv_w, conv_b, h0, table, out, x1_dram, mask_dram):
    f32, f16, bf16, i32 = mybir.dt.float32, mybir.dt.float16, mybir.dt.bfloat16, mybir.dt.int32
    ALU = mybir.AluOpType
    ACT = mybir.ActivationFunctionType
    AX = mybir.AxisListType.X

    x_v = x.rearrange("(b t) c h w -> b t c (h w)", b=SEQS)
    out_v = out.rearrange("(b t) c h w -> b t c (h w)", b=SEQS)
    h0_v = h0.rearrange("b c h w -> b c (h w)")
    w_v = conv_w.rearrange("o c h w -> o (c h w)")
    b_v = conv_b.rearrange("(g o a) -> g o a", g=3, a=1)

    ctx = ExitStack()
    with ctx:
        def sb(name, shape, dt=f32):
            return ctx.enter_context(nc.sbuf_tensor(name, shape, dt))

        def sem(name):
            return ctx.enter_context(nc.semaphore(name))

        staying = sb("staying", [128, C_END - C_STAY])
        spread = sb("spread", [128, 4, 128], bf16)
        ident16 = sb("ident16", [128, 128], f16)
        wst = sb("wst", [128, len(PASSES), 128], f16)
        bias = sb("bias", [128, 1])
        bias_half = sb("bias_half", [128, 1])
        unscale = sb("unscale", [128, 1])
        X = sb("X", [128, RESIDENT * TILES, PX])
        XN = sb("XN", [128, TILES, PX])
        XH = sb("XH", [128, TILES, PP], f16)
        XL = sb("XL", [128, TILES, PP], f16)
        U = sb("U", [128, 8, PP], f16)
        Z = sb("Z", [128, 8, SIDE * PAD], f16)
        V = sb("V", [128, 8, SIDE * PAD], f16)
        F = sb("F", [128, TILES, PX])
        S = sb("S", [128, TILES, PX])
        Tc = sb("Tc", [128, TILES, PX])
        H = sb("H", [128, TILES, PX])
        Y = sb("Y", [128, 2 * TILES, PX])
        MB = sb("MB", [128, TILES, PX], bf16)
        MK = sb("MK", [128, 4, HALF], bf16)
        bn1 = sb("bn1", [128, TILES, 12])
        bn2 = sb("bn2", [128, TILES, 12])
        mv = sb("mv", [128, 2 * TILES, 2])
        dm = sb("dm", [128, 2 * TILES])
        ve = sb("ve", [128, 2 * TILES])
        pw = sb("pw", [128, 2 * TILES])
        norm = sb("norm", [128, 2, 2 * TILES])
        power = sb("power", [128, 2 * TILES])
        scales = sb("scales", [128, 2 * TILES])
        idle = sb("idle", [128, 2])
        keep = sb("keep", [128, 4, K_END])
        kept = sb("kept", [128, GROUPS, K_END])
        small = sb("small", [128, 9])
        end = sb("end", [128, 13])
        inv = sb("inv", [128, 1])
        counts = sb("counts", [128, 7, GROUPS])
        padn = sb("padn", [128, GROUPS, TILES])
        prod = sb("prod", [128, GROUPS, TILES])
        first = sb("first", [128, GROUPS])
        coef_a = sb("coef_a", [128, GROUPS, TILES])
        coef_c = sb("coef_c", [128, GROUPS, TILES])

        conv = ctx.enter_context(nc.psum_tensor("conv", [128, 2, PX], f32))
        sums = ctx.enter_context(nc.psum_tensor("sums", [128, HALF], f32))
        stat = ctx.enter_context(nc.psum_tensor("stat", [128, HALF], f32))

        names = """consts_in h0_in weights_in prep zeroed transposed split_ready h_init
            xn_ready xh_ready xl_ready conv_done evac_done g_ready fh_ready h_ready x1_ready
            bn1_done bn2_done pairs_ready pairs_done link ve_ready power_done
            r_ready y_ready sums_done mask_ready ym_ready sq_done stored
            counts_ready counts_out fold folded pow_in pow_out coef_ready
            spread_in weights_laid bc2_done gain_ready t_done first_fixed out0_ready out1_ready""".split()
        s = {n: sem(n) for n in names}
        loaded = [sem(f"loaded{n}") for n in range(XRING)]
        copied = [[sem(f"copied{p}{image}") for image in range(2)] for p in range(2)]
        mask_out = [sem(f"mask_out{p}") for p in range(2)]
        out_stored = [sem(f"out_stored{n}") for n in range(4)]
        masks_in = [sem(f"masks_in{n}") for n in range(4)]
        early_in = [sem(f"early_in{n}") for n in range(EARLY)]
        back_in = [sem(f"back_in{n}") for n in range(RESIDENT)]

        def has_statistics(g):
            return (g + 2).exists() or (g + -1).exists()

        def wprep(p):
            return conv[:, 0, :].bitcast(f16)[:, 128 * p:128 * (p + 1)]

        def results(p):
            return (F[:, :, :], S[:, :, :], Y[:, 0:TILES, :], Y[:, TILES:2 * TILES, :])[p.slot(4)]

        def group_at(p):
            return p + -RESIDENT if p.i is not None or p.plus >= RESIDENT else p + (GROUPS - RESIDENT)

        def flat(t):
            return t[:, :, :].rearrange("p a b -> p (a b)").bitcast(f32)

        def early_tiles(n):
            if n == 0:
                return [XN[:, :, :].rearrange("p k x -> p (k x)")]
            if n == 1:
                return [flat(XH)[:, 0:PX], flat(XL)[:, 0:PX]]
            if n >= 8:
                return [(Tc, H)[n - 8][:, :, :].rearrange("p k x -> p (k x)")]
            at = TILES * PX * (n % 2)
            return [flat((U, Z, V)[n // 2 - 1])[:, at:at + TILES * PX]]

        def is_resident(p):
            return p.i is None and p.plus < RESIDENT

        def is_early(p):
            return p.i is None and RESIDENT <= p.plus < LATER

        def wait_x1(engine, p):
            if is_early(p):
                n = p.plus - RESIDENT
                wait(engine, early_in[n], 16 * len(early_tiles(n)))
            elif not is_resident(p):
                back = p + -LATER
                wait(engine, back_in[back.slot(RESIDENT)], back.round(RESIDENT, 16, 16))

        def x1_group(p):
            slot = TILES * (p if is_resident(p) else p + -LATER).slot(RESIDENT)
            return X[:, slot:slot + TILES, :]

        def x1_tile(p, k):
            if not is_early(p):
                return x1_group(p)[:, k, :]
            pieces = early_tiles(p.plus - RESIDENT)
            return pieces[k] if len(pieces) == TILES else pieces[0][:, k * PX:(k + 1) * PX]

        def x_slot(g):
            return XRING + g.plus - (GROUPS - LAST) if g.i is None and g.plus >= GROUPS - LAST else g.slot(XRING)

        def x_tile(g, k):
            return X[:, TILES * x_slot(g) + k, :]

        def step_of(v, g):
            if g.i is None:
                return v[g.plus]
            return v[bass.ds(g.value(1), 1)].rearrange("a c p -> (a c) p")

        def images_of(v, g, image):
            v = v[image::2]
            if g.i is None:
                return v[:, g.plus].rearrange("k c p -> c k p")
            return v[:, bass.ds(g.value(1), 1)].rearrange("k a c p -> (a c) k p")

        def operand_slot(g, image, k):
            return 4 * g.slot(2) + 2 * image + k

        def kept_of(g, column=None, t=kept):
            cols = slice(None) if column is None else slice(column, column + 1)
            if g.i is None:
                return t[:, g.plus, cols]
            return t[:, bass.ds(g.value(1), 1), cols].rearrange("p a b -> p (a b)")

        def keep_of(g, column, n):
            if keeps_directly(g):
                return kept[:, g.plus, column:column + n]
            return keep[:, g.slot(4), column:column + n]

        def keeps_directly(g):
            return g.i is None and g.plus >= LOOP_END - 1

        def group_of_x(g):
            slot = TILES * x_slot(g)
            return X[:, slot:slot + TILES, :].rearrange("p k x -> p (k x)")

        def mask_rows(slot):
            return MK[0:128:16, slot, :]

        const = lambda column, width: staying[:, column - C_STAY:column - C_STAY + width]
        once = X[:, TILES * (RESIDENT - 1) - 1, 0:C_STAY]
        WT = TILES * (RESIDENT - 1)
        inner = lambda t, k: t[:, k, :].rearrange("p (a b) -> p a b", b=PAD)[:, 1:1 + SIDE, 1:1 + SIDE]
        square = lambda ap: ap.rearrange("p (a b) -> p a b", b=SIDE)
        rows_of = lambda image: slice(CH * image, CH * (image + 1))

        block = ctx.enter_context(nc.Block())

        @block.sync
        def _(sp):
            def wait_all(*pairs):
                pairs = [(semaphore, v if isinstance(v, int) else sp.snap(sp.to_reg(v))) for semaphore, v in pairs]
                if any(not isinstance(value, int) for _, value in pairs):
                    sp.wait_ge(s["consts_in"], 16)
                for semaphore, value in pairs:
                    wait(sp, semaphore, value)

            def load(g):
                if not g.exists():
                    return
                if x_slot(g) < XRING:
                    wait_all((s["y_ready"], (g + -XRING).value(TILES, TILES)),
                             (s["stored"], (g + -XRING).value(16, 16)))
                slot = TILES * x_slot(g)
                for image in range(2):
                    sp.dma_start(X[rows_of(image), slot:slot + TILES, :], images_of(x_v, g, image))\
                        .then_inc(loaded[g.slot(XRING)], 16)

            def copies(g):
                if not g.exists():
                    return
                wait_all((s["xl_ready"], g.value(TILES, TILES)),
                         (s["conv_done"], (g + -2).value(4, 4)))
                n, used, below = SIDE * PAD, SIDE * PAD - 2, 2 * PAD
                for image in range(2):
                    done, slot = copied[g.slot(2)][image], operand_slot(g, image, 0)
                    both, of = slice(slot, slot + TILES), rows_of(image)
                    sp.dma_start(U[0:CH, both, :], XH[of, :, :]).then_inc(done, 16)
                    sp.dma_start(U[CH:128, both, :], XL[of, :, :]).then_inc(done, 16)
                    sp.dma_start(Z[0:CH, both, 0:n], XH[of, :, 0:n]).then_inc(done, 16)
                    sp.dma_start(Z[CH:128, both, 0:n], XH[of, :, PAD:PAD + n]).then_inc(done, 16)
                    sp.dma_start(V[0:CH, both, 0:used], XH[of, :, below:below + used]).then_inc(done, 16)
                    sp.dma_start(V[CH:128, both, 0:used], XH[of, :, below + 1:below + 1 + used]).then_inc(done, 16)

            def store(g):
                if not g.exists() or (g.i is None and g.plus >= GROUPS - RESIDENT):
                    return
                wait_all((s["x1_ready"], g.value(TILES, TILES)))
                sp.dma_start(step_of(x1_dram, g), group_of_x(g)).then_inc(s["stored"], 16)

            def store_mask(g):
                if not g.exists():
                    return
                wait_all((s["mask_ready"], g.value(1, 1)))
                sp.dma_start(step_of(mask_dram, g), mask_rows(g.slot(2))).then_inc(mask_out[g.slot(2)], 16)

            def spread_mask(g):
                if not g.exists():
                    return
                wait_all((mask_out[g.slot(2)], g.round(2, 16, 16)),
                         (s["ym_ready"], (g + -1).value(TILES, TILES)))
                rows = step_of(mask_dram, g).rearrange("(c i) x -> i c x", i=2)
                for image in range(2):
                    sp.dma_start(MB[rows_of(image), :, :].rearrange("p k x -> p (k x)")
                                 .rearrange("p (c x) -> p c x", x=HALF),
                                 rows[image:image + 1].broadcast_to([CH, 2 * TILES, HALF]))\
                        .then_inc(s["spread_in"], 16)

            def step(g):
                copies(g + 1)
                store_mask(g + -2)
                store(g + -1)
                load(g + 3)
                spread_mask(g + -2)

            def fetch_early(n):
                pieces = early_tiles(n)
                width = TILES * PX // len(pieces)
                for k, at in enumerate(pieces):
                    sp.dma_start(at, x1_dram[n, :, k * width:(k + 1) * width]).then_inc(early_in[n], 16)

            load(At(None, 0))
            sp.dma_start(staying[:, :], table[:, C_STAY:]).then_inc(s["consts_in"], 16)
            taps = CH * TAPS
            sp.dma_start(once, table[:, 0:C_STAY]).then_inc(s["weights_in"], 16)
            sp.dma_start(X[0:CH, WT, 0:taps], w_v[0:CH, :]).then_inc(s["weights_in"], 16)
            sp.dma_start(X[0:CH, WT + 1, 0:taps], w_v[CH:2 * CH, :]).then_inc(s["weights_in"], 16)
            sp.dma_start(X[CH:128, WT, 0:taps], w_v[2 * CH:3 * CH, :]).then_inc(s["weights_in"], 16)
            sp.dma_start(small[0:CH, 0:1], b_v[0]).then_inc(s["weights_in"], 16)
            sp.dma_start(small[0:CH, 1:2], b_v[1]).then_inc(s["weights_in"], 16)
            sp.dma_start(small[CH:128, 0:1], b_v[2]).then_inc(s["weights_in"], 16)
            load(At(None, 1))
            for seq in range(SEQS):
                sp.dma_start(H[rows_of(seq % 2), seq // 2, :], h0_v[seq]).then_inc(s["h0_in"], 16)
            for n in range(-1, UNROLL):
                step(At(None, n))
            with sp.Fori(0, LOOPS) as i:
                for q in range(UNROLL):
                    step(At(i, UNROLL + q))
            for n in range(LOOP_END, GROUPS - 1):
                step(At(None, n))
            sp.wait_ge(s["stored"], 16 * (GROUPS - RESIDENT))
            for p in range(2):
                for image in range(2):
                    sp.wait_ge(copied[p][image], 16 * COPIES * (GROUPS // 2))
            for n in range(2):
                fetch_early(n)
            step(At(None, GROUPS - 1))
            sp.wait_ge(s["conv_done"], 2 * NT)
            for n in range(2, 5):
                fetch_early(n)
            step(At(None, GROUPS))
            step(At(None, GROUPS + 1))

            for p in range(2):
                sp.wait_ge(mask_out[p], 16 * (GROUPS // 2))

            def fetch_masks(p):
                if not p.exists():
                    return
                before = (p + -4).value(TILES, TILES)
                wait_all((s["bc2_done"], before))
                sp.dma_start(mask_rows(p.slot(4)), step_of(mask_dram, group_at(p))).then_inc(masks_in[p.slot(4)], 16)

            def fetch_x1(p):
                if not p.exists():
                    return
                again = p.i is not None or p.plus >= LATER + RESIDENT
                last = p + -(RESIDENT if again else LATER)
                wait_all((s["t_done"], last.value(TILES, TILES)))
                sp.dma_start(x1_group(p).rearrange("p k x -> p (k x)"), step_of(x1_dram, group_at(p)))\
                    .then_inc(back_in[(p + -LATER).slot(RESIDENT)], 16)

            def put(p):
                wait_all((s["out0_ready"], p.value(1, 1)), (s["out1_ready"], p.value(1, 1)))
                for image in range(2):
                    sp.dma_start(images_of(out_v, group_at(p), image), results(p)[rows_of(image)])\
                        .then_inc(out_stored[p.slot(4)], 16)

            for n in range(3):
                fetch_masks(At(None, n))
            for n in range(5, EARLY):
                fetch_early(n)
            for n in range(LATER):
                fetch_masks(At(None, n + 3))
                if n < RESIDENT:
                    fetch_x1(At(None, LATER + n))
                put(At(None, n))
            fetch_masks(At(None, LATER + 3))
            put(At(None, LATER))
            with sp.Fori(0, 4) as i:
                for q in range(RESIDENT):
                    p = At(i, LATER + 1 + q, times=RESIDENT)
                    fetch_masks(p + 3)
                    fetch_x1(p + 7)
                    put(p)
            for n in range(LATER + 1 + 4 * RESIDENT, GROUPS):
                fetch_masks(At(None, n + 3))
                fetch_x1(At(None, n + 7))
                put(At(None, n))
            for stored in out_stored:
                sp.wait_ge(stored, 32 * (GROUPS // 4))

        @block.tensor
        def _(pe):
            mm = nc.tensor.matmul
            pe.wait_ge(s["consts_in"], 16)

            def unit(g, k, image):
                if not g.exists():
                    return
                if k == 0:
                    wait(pe, copied[g.slot(2)][image], g.round(2, 16 * COPIES, 16 * COPIES))
                wait(pe, s["evac_done"], g.value(4, 2 * k + image - 1))
                slot = operand_slot(g, image, k)
                for p, (operand, _, tap, other) in enumerate(PASSES):
                    (ky, kx), (ky2, kx2) = divmod(tap, 3), divmod(other, 3)
                    above = 2 if operand == "columns" else 0
                    padded = dict(parts=U, rows=Z, columns=V)[operand][:, slot, :].rearrange("p (a b) -> p a b", b=PAD)
                    left, right = int(kx == kx2 == 0), SIDE - int(kx == kx2 == 2)
                    for h in range(2):
                        top, bottom = h * ROWS, (h + 1) * ROWS
                        if h == 0 and ky == ky2 == 0:
                            top += 1
                        if h == 1 and ky == ky2 == 2:
                            bottom -= 1
                        last = mm(square(conv[:, image, :])[:, top:bottom, left:right], wst[:, p, :],
                                  padded[:, top + ky - above:bottom + ky - above, left + kx:right + kx],
                                  start=(p == 0), stop=(p == len(PASSES) - 1))
                last.then_inc(s["conv_done"], 1)

            def average(g):
                if not has_statistics(g):
                    return
                wait(pe, s["pairs_ready"], g.value(1, 3))
                wait(pe, s["ve_ready"], g.value(1, 2))
                mm(stat[:, 0:4 * TILES], const(C_PAIR, 128), mv[:, :, :].rearrange("p k m -> p (k m)"),
                   start=True, stop=True).then_inc(s["pairs_done"], 1)

            def channel_sums(g):
                if not g.exists():
                    return
                wait(pe, s["y_ready"], g.value(TILES, TILES))
                wait(pe, s["mask_ready"], g.value(1, 0))
                for chunk in range(4):
                    k, h = divmod(chunk, 2)
                    last = mm(sums[32 * chunk:32 * chunk + 32, :], const(C_SUM, 32),
                              Y[:, TILES * g.slot(2) + k, h * HALF:(h + 1) * HALF], start=True, stop=True)
                last.then_inc(s["sums_done"], 1)

            def step(g):
                unit(g, 0, 0)
                channel_sums(g + -2)
                unit(g, 0, 1)
                unit(g, 1, 0)
                average(g)
                unit(g, 1, 1)

            step(At(None, -2))
            step(At(None, -1))
            pe.wait_ge(s["split_ready"], 1)
            split = Tc[:, 0, :].bitcast(f16)
            for p, (_, low, first_tap, next_tap) in enumerate(PASSES):
                part = split[:, low * 1024:low * 1024 + CH * TAPS].rearrange("p (c t) -> p t c", t=TAPS)
                for n, tap in enumerate((first_tap, next_tap)):
                    last = nc.tensor.transpose(wprep(p)[CH * n:CH * (n + 1), :], part[:, tap, :], ident16[:, :])
            last.then_inc(s["transposed"], 1)
            pe.wait_ge(s["weights_laid"], 1)
            for n in range(UNROLL):
                step(At(None, n))
            with pe.Fori(0, LOOPS) as i:
                for q in range(UNROLL):
                    step(At(i, UNROLL + q))
            for n in range(LOOP_END, GROUPS + 2):
                step(At(None, n))

            pe.wait_ge(s["counts_ready"], 1)
            for n in range(6):
                mm(stat[:, GROUPS * n:GROUPS * (n + 1)], const(C_OWN + 128 * n, 128),
                   kept[:, :, K_COUNT], start=True, stop=True)
            mm(stat[:, GROUPS * 6:GROUPS * 7], const(C_ROW, 128), kept[:, :, K_COUNT],
               start=True, stop=True).then_inc(s["counts_out"], 1)
            pe.wait_ge(s["fold"], 1)
            mm(sums[:, 0:2], const(C_FOLD, 128), end[:, 4:6], start=True, stop=True)\
                .then_inc(s["folded"], 1)

            def spread_again(p):
                for k in range(TILES):
                    if k == 0:
                        wait(pe, s["first_fixed"], p.value(1, 1))
                    wait(pe, s["gain_ready"], p.value(TILES, k - 1))
                    for h in range(2):
                        last = mm(conv[:, k, h * HALF:(h + 1) * HALF], spread[:, 2 * k + h, :],
                                  MK[:, p.slot(4), :], start=True, stop=True)
                    last.then_inc(s["bc2_done"], 1)

            for n in range(4):
                spread_again(At(None, n))
            with pe.Fori(0, 15) as i:
                for q in range(4):
                    spread_again(At(i, 4 + q))

        @block.scalar
        def _(act):
            def high(g, k):
                if not g.exists():
                    return
                wait(act, s["xn_ready"], g.value(TILES, k + 1))
                before = g + -1
                for image in range(2):
                    wait(act, copied[before.slot(2)][image], before.round(2, 16 * COPIES, 16 * COPIES))
                nc.scalar.activation(inner(XH, k), square(XN[:, k, :]), ACT.Copy).then_inc(s["xh_ready"], 1)

            def gates(g, k, image):
                if not g.exists():
                    return
                wait(act, s["conv_done"], g.value(4, 2 * k + image + 1))
                wait(act, s["h_ready"], g.value(TILES, k - TILES + 1))
                to, a, b = rows_of(image), slice(0, CH), slice(CH, 128)
                nc.scalar.activation(F[to, k, :], conv[a, image, :], ACT.Sigmoid, bias=bias[a, :], scale=unscale[a, :])
                nc.scalar.activation(S[to, k, :], conv[b, image, :], ACT.Sigmoid, bias=bias[b, :], scale=unscale[b, :])
                nc.scalar.activation(Tc[to, k, :], conv[b, image, :], ACT.Identity, bias=bias_half[b, :],
                                     scale=unscale[b, :]).then_inc(s["evac_done"], 1)

            def squares(g, k):
                if not g.exists():
                    return
                wait(act, s["ym_ready"], g.value(TILES, k + 1))
                at = Y[:, TILES * g.slot(2) + k, :]
                nc.scalar.activation(at, at, ACT.Square, accum_out=keep_of(g, K_S2 + k, 1))\
                    .then_inc(s["sq_done"], 1)

            def step(g):
                gates(g + -1, 1, 1)
                high(g + 1, 0)
                high(g + 1, 1)
                gates(g, 0, 0)
                gates(g, 0, 1)
                squares(g + -3, 0)
                gates(g, 1, 0)
                squares(g + -3, 1)

            act.wait_ge(s["zeroed"], 1)
            step(At(None, -1))
            act.wait_ge(s["h0_in"], 64)
            for k in range(TILES):
                nc.scalar.activation(S[:, k, :], H[:, k, :], ACT.Sigmoid).then_inc(s["h_init"], 1)
            for n in range(UNROLL):
                step(At(None, n))
            with act.Fori(0, LOOPS) as i:
                for q in range(UNROLL):
                    step(At(i, UNROLL + q))
            for n in range(LOOP_END, GROUPS + 3):
                step(At(None, n))

            act.wait_ge(s["coef_ready"], 1)
            act.wait_ge(s["sq_done"], NT)

            def gain(p):
                g = group_at(p)
                for k in range(TILES):
                    wait(act, s["bc2_done"], p.value(TILES, k + 1))
                    if k == 0:
                        wait(act, out_stored[p.slot(4)], (p + -4).round(4, 32, 32))
                    nc.scalar.activation(results(p)[:, k, :], conv[:, k, :], ACT.Identity,
                                         scale=kept_of(g, k, coef_c), bias=kept_of(g, k, coef_a))\
                        .then_inc(s["gain_ready"], 1)

            def add_mean(p):
                if not p.exists():
                    return
                wait(act, s["t_done"], p.value(TILES, TILES))
                at = results(p)[:, 1, :]
                nc.scalar.activation(at, at, ACT.Identity, bias=kept_of(group_at(p), K_MEAN + 1))\
                    .then_inc(s["out1_ready"], 1)

            for n in range(LATER + 1):
                gain(At(None, n))
                add_mean(At(None, n - 1))
            with act.Fori(0, 5) as i:
                for q in range(RESIDENT):
                    p = At(i, LATER + 1 + q, times=RESIDENT)
                    gain(p)
                    add_mean(p + -1)
            for n in range(LATER + 1 + 5 * RESIDENT, GROUPS):
                gain(At(None, n))
                add_mean(At(None, n - 1))
            add_mean(At(None, GROUPS - 1))

        @block.gpsimd
        def _(pool):
            nc.gpsimd.memset(power[:, :], -0.5)
            nc.gpsimd.memset(scales[:, 0:TILES], XSCALE)
            nc.gpsimd.memset(scales[:, TILES:2 * TILES], 1.0)
            nc.gpsimd.memset(mv[:, :, :], 0.0)
            nc.gpsimd.memset(XH[:, :, :], 0.0)
            nc.gpsimd.memset(XL[:, :, :], 0.0)
            nc.gpsimd.memset(MK[:, :, :], 0.0).then_inc(s["zeroed"], 1)
            pool.wait_ge(s["zeroed"], 1)

            def low(g, k):
                if not g.exists():
                    return
                wait(pool, s["xh_ready"], g.value(TILES, k + 1))
                before = g + -1
                for image in range(2):
                    wait(pool, copied[before.slot(2)][image], before.round(2, 16 * COPIES, 16 * COPIES))
                nc.gpsimd.tensor_tensor(inner(XL, k), square(XN[:, k, :]), inner(XH, k), ALU.subtract)\
                    .then_inc(s["xl_ready"], 1)

            def add_h(g, k):
                if not g.exists():
                    return
                wait(pool, s["h_ready"], g.value(TILES, k + 1))
                at = x_tile(g, k)
                nc.gpsimd.tensor_tensor(at, at, H[:, k, :], ALU.add).then_inc(s["x1_ready"], 1)

            def rstd(g):
                if not has_statistics(g):
                    return
                wait(pool, s["ve_ready"], g.value(1, 3))
                nc.gpsimd.tensor_tensor(pw[:, :], ve[:, :], power[:, :], ALU.pow).then_inc(s["power_done"], 1)
                wait(pool, s["power_done"], g.value(1, 3))
                nc.gpsimd.tensor_tensor(norm[:, 1, :], pw[:, :], scales[:, :], ALU.mult).then_inc(s["r_ready"], 1)

            def step(g):
                low(g + 1, 0)
                low(g + 1, 1)
                add_h(g + -1, 1)
                rstd(g)
                add_h(g, 0)

            for n in range(-2, UNROLL):
                step(At(None, n))
            with pool.Fori(0, LOOPS) as i:
                for q in range(UNROLL):
                    step(At(i, UNROLL + q))
            for n in range(LOOP_END, GROUPS + 1):
                step(At(None, n))
            pool.wait_ge(s["pow_in"], 1)
            nc.gpsimd.tensor_tensor(inv[:, :], end[:, 12:13], power[:, 0:1], ALU.pow)\
                .then_inc(s["pow_out"], 1)

        @block.vector
        def _(dve):
            v = nc.vector
            prepared = [0]

            def then(ins):
                prepared[0] += 1
                ins.then_inc(s["prep"], 1)
                dve.wait_ge(s["prep"], prepared[0])

            v.memset(idle[:, :], 0.0)
            dve.wait_ge(s["consts_in"], 16)

            def stats1(g):
                if not g.exists():
                    return
                dve.wait_ge(loaded[g.slot(XRING)], g.round(XRING, 32, 32))
                for k in range(TILES):
                    at = x_tile(g, k)
                    v.bn_stats(bn1[:, k, 0:6], at[:, 0:HALF])
                    v.bn_stats(bn1[:, k, 6:12], at[:, HALF:PX]).then_inc(s["bn1_done"], 1)
                wait(dve, s["bn1_done"], g.value(TILES, TILES))
                v.tensor_copy(idle[:, 0:1], idle[:, 1:2])
                for k in range(TILES):
                    last = v.bn_aggr(mv[:, k, :], bn1[:, k, :])
                return last

            def stats2(g):
                if not g.exists():
                    return
                for k in range(TILES):
                    wait(dve, s["x1_ready"], g.value(TILES, k + 1))
                    at = x_tile(g, k)
                    v.bn_stats(bn2[:, k, 0:6], at[:, 0:HALF])
                    v.bn_stats(bn2[:, k, 6:12], at[:, HALF:PX]).then_inc(s["bn2_done"], 1)
                wait(dve, s["bn2_done"], g.value(TILES, TILES))
                v.tensor_copy(idle[:, 0:1], idle[:, 1:2])
                for k in range(TILES):
                    last = v.bn_aggr(mv[:, TILES + k, :], bn2[:, k, :])
                return last

            def statistics(g):
                made = [stats1(g + 2), stats2(g + -1)]
                if has_statistics(g):
                    (made[1] or made[0]).then_inc(s["pairs_ready"], 1)

            def finish(g):
                if not has_statistics(g):
                    return
                wait(dve, s["pairs_done"], g.value(1, 3))
                wait(dve, s["r_ready"], g.value(1, 2))
                pair = stat[:, 0:4 * TILES].rearrange("p (k m) -> p m k", m=2)
                v.tensor_copy(norm[:, 0, :], pair[:, 0, :])
                v.tensor_tensor(dm[:, :], mv[:, :, 0], pair[:, 0, :], ALU.subtract).then_inc(s["link"], 1)
                wait(dve, s["link"], g.value(2, 5))
                v.tensor_tensor(dm[:, :], dm[:, :], dm[:, :], ALU.mult).then_inc(s["link"], 1)
                wait(dve, s["link"], g.value(2, 6))
                v.scalar_tensor_tensor(ve[:, :], dm[:, :], GN_EPS, pair[:, 1, :], ALU.add, ALU.add)\
                    .then_inc(s["ve_ready"], 1)

            def normalise1(g, k):
                if not g.exists():
                    return
                wait(dve, s["r_ready"], g.value(1, 1))
                wait(dve, s["xl_ready"], g.value(TILES, k - TILES + 1))
                v.tensor_scalar(XN[:, k, :], x_tile(g, k), norm[:, 0, k:k + 1], norm[:, 1, k:k + 1],
                                ALU.subtract, ALU.mult).then_inc(s["xn_ready"], 1)

            def recur(g, k):
                if not g.exists():
                    return
                wait(dve, s["evac_done"], g.value(4, 2 * k + 2))
                wait(dve, s["x1_ready"], g.value(TILES, k - TILES + 1))
                f, c, i = F[:, k, :], Tc[:, k, :], S[:, k, :]
                v.tensor_tensor(c, c, i, ALU.max).then_inc(s["g_ready"], 1)
                wait(dve, s["g_ready"], g.value(TILES, k + 1))
                v.scalar_tensor_tensor(i, f, 1.0, c, ALU.subtract, ALU.mult)
                v.tensor_tensor(f, f, H[:, k, :], ALU.mult).then_inc(s["fh_ready"], 1)
                wait(dve, s["fh_ready"], g.value(TILES, k + 1))
                v.tensor_tensor(H[:, k, :], f, i, ALU.subtract).then_inc(s["h_ready"], 1)

            def mask(g):
                if not g.exists():
                    return
                wait(dve, s["sums_done"], g.done(1))
                wait(dve, mask_out[g.slot(2)], (g + -2).round(2, 16, 16))
                v.tensor_scalar(MK[:, g.slot(2), :], sums[:, :], 0.0, None, ALU.not_equal, ALU.add,
                                accum_out=keep_of(g, K_COUNT, 1)).then_inc(s["mask_ready"], 1)

            def masked(g, k):
                if not g.exists():
                    return
                wait(dve, s["spread_in"], g.value(32, 32))
                at = Y[:, TILES * g.slot(2) + k, :]
                v.scalar_tensor_tensor(at, MB[:, k, :], 1.0, at, ALU.mult, ALU.mult,
                                       accum_out=keep_of(g, K_S1 + k, 1)).then_inc(s["ym_ready"], 1)

            def store_kept(g):
                if not g.exists() or keeps_directly(g):
                    return
                wait(dve, s["sq_done"], g.done(TILES))
                wait(dve, s["ym_ready"], g.done(TILES))
                v.tensor_copy(kept_of(g), keep[:, g.slot(4), :])

            def normalise2(g):
                if not g.exists():
                    return
                wait(dve, s["r_ready"], g.value(1, 4))
                Yg = Y[:, TILES * g.slot(2):TILES * g.slot(2) + TILES, :]
                for k in range(TILES):
                    wait(dve, s["sq_done"], (g + -2).value(TILES, k + 1))
                    mean, rstd = (norm[:, n, TILES + k:TILES + k + 1] for n in range(2))
                    v.tensor_scalar(Yg[:, k, :], x_tile(g, k), mean, rstd,
                                    ALU.subtract, ALU.mult).then_inc(s["y_ready"], 1)
                v.tensor_copy(keep_of(g, K_MEAN, 2 * TILES).rearrange("p (n k) -> p n k", n=2),
                              norm[:, :, TILES:2 * TILES])
                wait(dve, s["y_ready"], g.done(TILES))
                v.tensor_copy(keep_of(g, K_FIRST, TILES), Yg[:, :, 0])

            def step(g):
                normalise1(g + 1, 0)
                normalise1(g + 1, 1)
                recur(g + -1, 1)
                mask(g + -2)
                statistics(g)
                masked(g + -3, 0)
                recur(g, 0)
                finish(g)
                masked(g + -3, 1)
                store_kept(g + -4)
                normalise2(g + -1)

            dve.wait_ge(s["zeroed"], 1)
            step(At(None, -2))
            taps = CH * TAPS
            dve.wait_ge(s["weights_in"], 112)
            v.tensor_copy(ident16[:, :], once[:, C_IDENT:C_IDENT + 128])
            then(v.tensor_copy(spread[:, :, :].rearrange("p a b -> p (a b)"), once[:, C_SPREAD:C_SPREAD + 512]))
            w = X[:, WT, 0:taps]
            then(v.tensor_tensor(X[0:CH, WT, 0:taps], X[0:CH, WT, 0:taps], X[0:CH, WT + 1, 0:taps], ALU.subtract))
            then(v.tensor_tensor(small[0:CH, 0:1], small[0:CH, 0:1], small[0:CH, 1:2], ALU.subtract))
            step(At(None, -1))
            v.tensor_copy(bias[:, :], small[:, 0:1])
            then(v.tensor_scalar(bias_half[:, :], small[:, 0:1], 0.5, None, ALU.add))
            then(v.tensor_reduce(small[:, 2:3], w, AX, ALU.max, apply_absolute_value=True))
            then(v.tensor_scalar(small[:, 2:3], small[:, 2:3], 1e-30, 1e30, ALU.max, ALU.min))
            then(v.tensor_scalar(small[:, 3:4].bitcast(i32), small[:, 2:3].bitcast(i32), 0x7F800000, None,
                                 ALU.bitwise_and))
            v.tensor_scalar(unscale[:, :], small[:, 3:4], 1.0 / (WSCALE * XSCALE), None, ALU.mult)
            then(v.reciprocal(small[:, 7:8], small[:, 3:4]))
            then(v.tensor_scalar(w, w, small[:, 7:8], WSCALE, ALU.mult, ALU.mult))
            split = Tc[:, 0, :].bitcast(f16)
            then(v.tensor_copy(split[:, 0:taps], w))
            v.tensor_tensor(split[:, 1024:1024 + taps], w, split[:, 0:taps], ALU.subtract).then_inc(s["split_ready"], 1)
            dve.wait_ge(s["transposed"], 1)
            for p in range(len(PASSES)):
                last = v.tensor_copy(wst[:, p, :], wprep(p))
            last.then_inc(s["weights_laid"], 1)
            dve.wait_ge(s["h_init"], TILES)
            for k in range(TILES):
                last = v.scalar_tensor_tensor(H[:, k, :], H[:, k, :], 0.5, S[:, k, :], ALU.add, ALU.max)
            then(last)
            for n in range(UNROLL):
                step(At(None, n))
            with dve.Fori(0, LOOPS) as i:
                for q in range(UNROLL):
                    step(At(i, UNROLL + q))
            for n in range(LOOP_END, GROUPS + 2):
                step(At(None, n))

            v.tensor_copy(end[:, 0:1], kept[:, 0, 0:1]).then_inc(s["counts_ready"], 1)
            dve.wait_ge(s["counts_ready"], 1)
            rstd = kept[:, :, K_RSTD:K_RSTD + TILES]
            v.tensor_scalar(coef_a[:, :, :], rstd, 1.0, None, ALU.add)
            dve.wait_ge(s["counts_out"], 1)
            then(v.tensor_copy(counts[:, :, :].rearrange("p a b -> p (a b)"), stat[:, 0:7 * GROUPS]))
            then(v.reduce_max(end[:, 0:1], counts[:, 2:6, :].rearrange("p a b -> p (a b)"), AX))
            most = end[:, 0:1]
            v.tensor_scalar(first[:, :], counts[:, 6, :], most, const(C_FIRST, 1), ALU.is_lt, ALU.mult)
            v.tensor_scalar(end[:, 6:7], most, float(SEQS * STEPS), 1.0, ALU.mult, ALU.max)
            then(v.tensor_scalar(padn[:, :, :], counts[:, 0:2, :].rearrange("p k g -> p g k"), most, -1.0,
                                 ALU.subtract, ALU.mult))
            v.reciprocal(end[:, 11:12], end[:, 6:7])
            y0 = kept[:, :, K_FIRST:K_FIRST + TILES]
            then(v.scalar_tensor_tensor(prod[:, :, :], padn[:, :, :], 1.0, y0, ALU.mult, ALU.mult,
                                        accum_out=end[:, 2:3]))
            then(v.scalar_tensor_tensor(padn[:, :, :], prod[:, :, :], 1.0, y0, ALU.mult, ALU.mult,
                                        accum_out=end[:, 3:4]))
            step(At(None, GROUPS + 2))
            dve.wait_ge(s["ym_ready"], NT)
            v.tensor_reduce(end[:, 4:5], kept[:, :, K_S1:K_S1 + TILES], mybir.AxisListType.XY, ALU.add)
            dve.wait_ge(s["sq_done"], NT)
            then(v.tensor_reduce(end[:, 5:6], kept[:, :, K_S2:K_S2 + TILES], mybir.AxisListType.XY, ALU.add))
            then(v.tensor_tensor(end[:, 4:6], end[:, 4:6], end[:, 2:4], ALU.add))
            v.tensor_copy(end[:, 1:2], end[:, 4:5]).then_inc(s["fold"], 1)
            dve.wait_ge(s["folded"], 1)
            then(v.tensor_scalar(end[:, 8:10], sums[:, 0:2], end[:, 11:12], None, ALU.mult))
            then(v.tensor_tensor(end[:, 7:8], end[:, 8:9], end[:, 8:9], ALU.mult))
            then(v.tensor_tensor(end[:, 10:11], end[:, 9:10], end[:, 7:8], ALU.subtract))
            v.tensor_scalar(end[:, 12:13], end[:, 10:11], 0.0, BN_EPS, ALU.max, ALU.add).then_inc(s["pow_in"], 1)

            def fix_first(p):
                if not p.exists():
                    return
                wait(dve, masks_in[p.slot(4)], p.round(4, 16, 16))
                at, g = MK[:, p.slot(4), 0:1], group_at(p)
                has_pad = first[:, g.plus:g.plus + 1] if g.i is None else first[:, bass.ds(g.value(1), 1)]
                v.tensor_tensor(at, at, has_pad, ALU.max).then_inc(s["first_fixed"], 1)

            def scale(p):
                fix_first(p + 1)
                g = group_at(p)
                for k in range(TILES):
                    wait(dve, s["gain_ready"], p.value(TILES, k + 1))
                    if k == 0:
                        wait_x1(dve, p)
                    at = results(p)[:, k, :]
                    v.scalar_tensor_tensor(at, x1_tile(p, k), kept_of(g, K_MEAN + k), at, ALU.subtract, ALU.mult)\
                        .then_inc(s["t_done"], 1)
                wait(dve, s["t_done"], p.value(TILES, 1))
                at = results(p)[:, 0, :]
                v.tensor_scalar(at, at, kept_of(g, K_MEAN), None, ALU.add).then_inc(s["out0_ready"], 1)

            fix_first(At(None, 0))
            dve.wait_ge(s["pow_out"], 1)
            then(v.tensor_scalar(end[:, 10:11], inv[:, :], -1.0, None, ALU.add))
            v.tensor_scalar(coef_c[:, :, :], rstd, end[:, 10:11], None, ALU.mult).then_inc(s["coef_ready"], 1)
            for n in range(LATER):
                scale(At(None, n))
            with dve.Fori(0, 5) as i:
                for q in range(RESIDENT):
                    scale(At(i, LATER + q, times=RESIDENT))
            for n in range(LATER + 5 * RESIDENT, GROUPS):
                scale(At(None, n))


def kernel(**inputs):
    import numpy as np
    import concourse.bacc as bacc
    from concourse.bass_utils import run_bass_kernel_spmd

    nc = bacc.Bacc("TRN2", target_bir_lowering=False, num_devices=1)
    arrays, args = {}, []
    for name in ("x", "L0_conv_conv_w", "L0_conv_conv_b", "L0_conv_h0"):
        arrays["in_" + name] = np.ascontiguousarray(inputs[name])
    arrays["in_table"] = constant_table()
    for name, a in arrays.items():
        args.append(nc.dram_tensor(name, a.shape, mybir.dt.from_np(a.dtype), kind="ExternalInput").ap())
    out = nc.dram_tensor("out_dram", (SEQS * STEPS, CH, SIDE, SIDE), mybir.dt.float32, kind="ExternalOutput").ap()
    x1 = nc.dram_tensor("x1_dram", (GROUPS - RESIDENT, 128, TILES * PX), mybir.dt.float32, kind="Internal").ap()
    masks = nc.dram_tensor("mask_dram", (GROUPS, 8, HALF), mybir.dt.bfloat16, kind="Internal").ap()
    preact_kernel(nc, *args, out, x1, masks)
    r = run_bass_kernel_spmd(nc, [arrays], core_ids=[0])
    return r.results[0]["out_dram"]
```
